# Optimizing a Trainium2 kernel written in Bass

```python
import numpy as np
import jax
import jax.numpy as jnp

def _softmax(x, axis=-1):
    return jax.nn.softmax(x, axis=axis)

def _gelu(x):
    return jax.nn.gelu(x, approximate=True)

def _silu(x):
    return jax.nn.silu(x)

def _sigmoid(x):
    return jax.nn.sigmoid(x)

def _layernorm(x, axis=-1, eps=1e-05):
    m = jnp.mean(x, axis=axis, keepdims=True)
    v = jnp.var(x, axis=axis, keepdims=True)
    return (x - m) / jnp.sqrt(v + eps)

def _scatter_add(tgt, idx, src, axis=0):
    return tgt.at[idx].add(src)

def _segment_sum(src, seg, n):
    return jax.ops.segment_sum(src, seg, n)
kernel_name = 'mk_gnn_preln_d4_gnn_r16_a83d61'

def setup_inputs(seed: int=0):
    np.random.seed(seed)
    _w = jnp.asarray

    def _rec_inputs():
        import jax
        import jax.numpy as jnp
        _gk = jax.random.key(seed)
        x = -0.0003713 + 1 * jax.random.normal(jax.random.fold_in(_gk, 1), (3125, 128), jnp.float32)
        src = jax.random.randint(jax.random.fold_in(_gk, 2), (50000,), 0, 3125, jnp.int32)
        dst = jax.random.randint(jax.random.fold_in(_gk, 3), (50000,), 0, 3125, jnp.int32)
        _o = jnp.argsort(dst, stable=True)
        src = src[_o]
        dst = dst[_o]
        edge_weight = jax.random.uniform(jax.random.fold_in(_gk, 12), (50000,), jnp.float32, 0.0, 0.999998)
        return (x, src, dst, edge_weight)
    x, src, dst, edge_weight = _rec_inputs()

    def _L0_gnn_setup():
        import jax, jax.numpy as jnp
        import numpy as np
        N = 6250
        E = 62500
        F_IN = 128
        F_OUT = 64
        NHOP = 2

        def _xavier(k, shape, gain=1.414):
            fan_in, fan_out = shape
            std = gain * np.sqrt(2.0 / (fan_in + fan_out))
            return (jax.random.normal(k, shape) * std).astype(jnp.float32)

        def _spmm(row, col, val, v, n):
            return jax.ops.segment_sum(val[:, None] * v[col], row, num_segments=n)

        def _adaptive_enc(y, fc, bf):
            g = jax.nn.sigmoid(y @ fc + bf)
            return jnp.where(y < 0, 0.0, y) + g * jnp.where(y > 0, 0.0, y)
        key = jax.random.key(seed)
        ks = jax.random.split(key, 8)
        x = jax.random.normal(ks[0], (N, F_IN), jnp.float32)
        edge_index = jax.random.randint(ks[1], (2, E), 0, N)
        edge_attr = jax.random.uniform(ks[2], (E,), jnp.float32)
        W0 = _xavier(ks[3], (F_IN, F_OUT))
        W1 = _xavier(ks[4], (F_IN, F_OUT))
        b0 = jnp.zeros((F_OUT,), jnp.float32)
        b1 = jnp.zeros((F_OUT,), jnp.float32)
        fc0 = _xavier(ks[5], (F_OUT, 1))
        fc1 = _xavier(ks[6], (F_OUT, 1))
        bf0 = jnp.zeros((1,), jnp.float32)
        bf1 = jnp.zeros((1,), jnp.float32)
        return dict(x=x, edge_index=edge_index, edge_attr=edge_attr, W0=W0, b0=b0, W1=W1, b1=b1, fc0=fc0, bf0=bf0, fc1=fc1, bf1=bf1)
    _L0_gnn_all = _L0_gnn_setup()
    _L0_gnn_in = {k: v for k, v in _L0_gnn_all.items() if k in ('W0', 'b0', 'W1', 'b1', 'fc0', 'bf0', 'fc1', 'bf1')}
    del _L0_gnn_all

    def _L1_gnn_setup():
        import jax, jax.numpy as jnp
        import numpy as np
        N = 2500
        E = 40000
        IN = 128
        H = 4
        C = 32
        key = jax.random.key(seed)
        ks = jax.random.split(key, 5)
        x = jax.random.normal(ks[0], (N, IN), dtype=jnp.float32)
        edge_index = jax.random.randint(ks[1], (2, E), 0, N, dtype=jnp.int64)
        W_lin = jax.random.normal(ks[2], (IN, H * C), dtype=jnp.float32) * 0.05
        b_lin = jnp.zeros((H * C,), dtype=jnp.float32)
        W_att = jax.random.normal(ks[3], (2 * H * C, H), dtype=jnp.float32) * 0.05
        b_att = jnp.zeros((H,), dtype=jnp.float32)
        return {'x': x, 'edge_index': edge_index, 'W_lin': W_lin, 'b_lin': b_lin, 'W_att': W_att, 'b_att': b_att}
    _L1_gnn_all = _L1_gnn_setup()
    _L1_gnn_in = {k: v for k, v in _L1_gnn_all.items() if k in ('W_lin', 'b_lin', 'W_att', 'b_att')}
    del _L1_gnn_all

    def _L2_gnn_setup():
        import jax, jax.numpy as jnp
        import numpy as np
        N = 625
        E = 10000
        IN = 128
        H1, C1 = (4, 128)
        H2, C2 = (2, 128)

        def transformer_conv(x, src, dst, Wq, bq, Wk, bk, Wv, bv, Ws, bs, H, C, concat):
            n = x.shape[0]
            q = (x @ Wq + bq).reshape(n, H, C)
            k = (x @ Wk + bk).reshape(n, H, C)
            v = (x @ Wv + bv).reshape(n, H, C)
            alpha = jnp.einsum('ehc,ehc->eh', q[dst], k[src]) / jnp.sqrt(jnp.float32(C))
            amax = jax.ops.segment_max(alpha, dst, num_segments=n)
            amax = jax.lax.stop_gradient(jnp.where(jnp.isfinite(amax), amax, 0.0))
            p = jnp.exp(alpha - amax[dst])
            denom = jax.ops.segment_sum(p, dst, num_segments=n) + 1e-16
            out = jax.ops.segment_sum(p[:, :, None] * v[src], dst, num_segments=n)
            out = out / denom[:, :, None]
            out = out.reshape(n, H * C) if concat else out.mean(axis=1)
            return out + x @ Ws + bs
        key = jax.random.key(seed)
        ks = jax.random.split(key, 20)
        w = lambda k, s: jax.random.normal(k, s, jnp.float32) * 0.02
        inp = {'x': jax.random.normal(ks[0], (N, IN), jnp.float32), 'edge_index': jax.random.randint(ks[1], (2, E), 0, N, jnp.int32), 'Wq1': w(ks[2], (IN, H1 * C1)), 'bq1': w(ks[3], (H1 * C1,)), 'Wk1': w(ks[4], (IN, H1 * C1)), 'bk1': w(ks[5], (H1 * C1,)), 'Wv1': w(ks[6], (IN, H1 * C1)), 'bv1': w(ks[7], (H1 * C1,)), 'Ws1': w(ks[8], (IN, H1 * C1)), 'bs1': w(ks[9], (H1 * C1,)), 'Wq2': w(ks[10], (H1 * C1, H2 * C2)), 'bq2': w(ks[11], (H2 * C2,)), 'Wk2': w(ks[12], (H1 * C1, H2 * C2)), 'bk2': w(ks[13], (H2 * C2,)), 'Wv2': w(ks[14], (H1 * C1, H2 * C2)), 'bv2': w(ks[15], (H2 * C2,)), 'Ws2': w(ks[16], (H1 * C1, C2)), 'bs2': w(ks[17], (C2,))}
        return inp
    _L2_gnn_all = _L2_gnn_setup()
    _L2_gnn_in = {k: v for k, v in _L2_gnn_all.items() if k in ('Wq1', 'bq1', 'Wk1', 'bk1', 'Wv1', 'bv1', 'Ws1', 'bs1', 'Wq2', 'bq2', 'Wk2', 'bk2', 'Wv2', 'bv2', 'Ws2', 'bs2')}
    del _L2_gnn_all

    def _L3_gnn_setup():
        import jax, jax.numpy as jnp
        import numpy as np
        N_NODES = 3125
        N_EDGES = 37500
        IN_DIM = 128
        OUT_DIM = 128
        EPS = 1e-05

        def _layernorm(x, gamma, beta):
            mu = jnp.mean(x, axis=-1, keepdims=True)
            var = jnp.mean(jnp.square(x - mu), axis=-1, keepdims=True)
            return (x - mu) * jax.lax.rsqrt(var + EPS) * gamma + beta
        key = jax.random.key(seed)
        k1, k2, k3 = jax.random.split(key, 3)
        h = jax.random.normal(k1, (N_NODES, IN_DIM), dtype=jnp.float32)
        edge_index = jax.random.randint(k2, (2, N_EDGES), 0, N_NODES, dtype=jnp.int64)
        ln_gamma = jnp.ones((IN_DIM,), dtype=jnp.float32)
        ln_beta = jnp.zeros((IN_DIM,), dtype=jnp.float32)
        W = jax.random.normal(k3, (OUT_DIM, 2 * IN_DIM), dtype=jnp.float32) * (1.0 / np.sqrt(2 * IN_DIM))
        b = jnp.zeros((OUT_DIM,), dtype=jnp.float32)
        return {'h': h, 'edge_index': edge_index, 'ln_gamma': ln_gamma, 'ln_beta': ln_beta, 'W': W, 'b': b}
    _L3_gnn_all = _L3_gnn_setup()
    _L3_gnn_in = {k: v for k, v in _L3_gnn_all.items() if k in ('ln_gamma', 'ln_beta', 'W', 'b')}
    del _L3_gnn_all
    return {'x': x, 'src': src, 'dst': dst, 'edge_weight': edge_weight, 'L0_gnn_W0': _L0_gnn_in['W0'], 'L0_gnn_b0': _L0_gnn_in['b0'], 'L0_gnn_W1': _L0_gnn_in['W1'], 'L0_gnn_b1': _L0_gnn_in['b1'], 'L0_gnn_fc0': _L0_gnn_in['fc0'], 'L0_gnn_bf0': _L0_gnn_in['bf0'], 'L0_gnn_fc1': _L0_gnn_in['fc1'], 'L0_gnn_bf1': _L0_gnn_in['bf1'], 'L1_gnn_W_lin': _L1_gnn_in['W_lin'], 'L1_gnn_b_lin': _L1_gnn_in['b_lin'], 'L1_gnn_W_att': _L1_gnn_in['W_att'], 'L1_gnn_b_att': _L1_gnn_in['b_att'], 'L2_gnn_Wq1': _L2_gnn_in['Wq1'], 'L2_gnn_bq1': _L2_gnn_in['bq1'], 'L2_gnn_Wk1': _L2_gnn_in['Wk1'], 'L2_gnn_bk1': _L2_gnn_in['bk1'], 'L2_gnn_Wv1': _L2_gnn_in['Wv1'], 'L2_gnn_bv1': _L2_gnn_in['bv1'], 'L2_gnn_Ws1': _L2_gnn_in['Ws1'], 'L2_gnn_bs1': _L2_gnn_in['bs1'], 'L2_gnn_Wq2': _L2_gnn_in['Wq2'], 'L2_gnn_bq2': _L2_gnn_in['bq2'], 'L2_gnn_Wk2': _L2_gnn_in['Wk2'], 'L2_gnn_bk2': _L2_gnn_in['bk2'], 'L2_gnn_Wv2': _L2_gnn_in['Wv2'], 'L2_gnn_bv2': _L2_gnn_in['bv2'], 'L2_gnn_Ws2': _L2_gnn_in['Ws2'], 'L2_gnn_bs2': _L2_gnn_in['bs2'], 'L3_gnn_ln_gamma': _L3_gnn_in['ln_gamma'], 'L3_gnn_ln_beta': _L3_gnn_in['ln_beta'], 'L3_gnn_W': _L3_gnn_in['W'], 'L3_gnn_b': _L3_gnn_in['b']}

def reference(x, src, dst, edge_weight, L0_gnn_W0, L0_gnn_b0, L0_gnn_W1, L0_gnn_b1, L0_gnn_fc0, L0_gnn_bf0, L0_gnn_fc1, L0_gnn_bf1, L1_gnn_W_lin, L1_gnn_b_lin, L1_gnn_W_att, L1_gnn_b_att, L2_gnn_Wq1, L2_gnn_bq1, L2_gnn_Wk1, L2_gnn_bk1, L2_gnn_Wv1, L2_gnn_bv1, L2_gnn_Ws1, L2_gnn_bs1, L2_gnn_Wq2, L2_gnn_bq2, L2_gnn_Wk2, L2_gnn_bk2, L2_gnn_Wv2, L2_gnn_bv2, L2_gnn_Ws2, L2_gnn_bs2, L3_gnn_ln_gamma, L3_gnn_ln_beta, L3_gnn_W, L3_gnn_b):
    import jax
    import jax.numpy as jnp

    def _L0_gnn_ref(x, edge_index, edge_attr, W0, b0, W1, b1, fc0, bf0, fc1, bf1):
        import jax, jax.numpy as jnp
        import numpy as np
        N = 6250
        E = 62500
        F_IN = 128
        F_OUT = 64
        NHOP = 2

        def _xavier(k, shape, gain=1.414):
            fan_in, fan_out = shape
            std = gain * np.sqrt(2.0 / (fan_in + fan_out))
            return (jax.random.normal(k, shape) * std).astype(jnp.float32)

        def _spmm(row, col, val, v, n):
            return jax.ops.segment_sum(val[:, None] * v[col], row, num_segments=n)

        def _adaptive_enc(y, fc, bf):
            g = jax.nn.sigmoid(y @ fc + bf)
            return jnp.where(y < 0, 0.0, y) + g * jnp.where(y > 0, 0.0, y)
        n = x.shape[0]
        row, col = (edge_index[0], edge_index[1])
        ones = jnp.ones((n, 1), x.dtype)
        params = [(W0, b0, fc0, bf0), (W1, b1, fc1, bf1)]
        outs = []
        for hop in range(NHOP):
            W, b, fc, bf = params[hop]
            h = x @ W
            agg, deg = (h, ones)
            for _ in range(hop + 1):
                agg = _spmm(row, col, edge_attr, agg, n)
                deg = _spmm(row, col, edge_attr, deg, n)
            safe_deg = jnp.where(deg > 0, deg, 1.0)
            y = jnp.where(deg > 0, agg / safe_deg, 0.0)
            y = y + b
            outs.append(_adaptive_enc(y, fc, bf))
        return jnp.concatenate(outs, axis=1)

    def _L1_gnn_ref(x, edge_index, W_lin, b_lin, W_att, b_att):
        import jax, jax.numpy as jnp
        import numpy as np
        N = 2500
        E = 40000
        IN = 128
        H = 4
        C = 32
        n = x.shape[0]
        row, col = (edge_index[0], edge_index[1])
        xl = x @ W_lin + b_lin
        hc = xl.shape[1]
        s_i = xl @ W_att[:hc]
        s_j = xl @ W_att[hc:]
        alpha = s_i[row] + s_j[col] + b_att
        alpha = jnp.where(alpha >= 0, alpha, 0.2 * alpha)
        amax = jax.ops.segment_max(alpha, row, num_segments=n)
        alpha = jnp.exp(alpha - amax[row])
        asum = jax.ops.segment_sum(alpha, row, num_segments=n)
        alpha = alpha / (asum[row] + 1e-16)
        xh = xl.reshape(n, H, C)
        msg = alpha[:, :, None] * xh[row]
        out = jax.ops.segment_sum(msg, col, num_segments=n)
        deg = jax.ops.segment_sum(jnp.ones((row.shape[0],), xl.dtype), col, num_segments=n)
        out = jnp.where(deg[:, None, None] > 0, out, xh)
        return out.reshape(n, H * C)

    def _L2_gnn_ref(x, edge_index, Wq1, bq1, Wk1, bk1, Wv1, bv1, Ws1, bs1, Wq2, bq2, Wk2, bk2, Wv2, bv2, Ws2, bs2):
        import jax, jax.numpy as jnp
        import numpy as np
        N = 625
        E = 10000
        IN = 128
        H1, C1 = (4, 128)
        H2, C2 = (2, 128)

        def transformer_conv(x, src, dst, Wq, bq, Wk, bk, Wv, bv, Ws, bs, H, C, concat):
            n = x.shape[0]
            q = (x @ Wq + bq).reshape(n, H, C)
            k = (x @ Wk + bk).reshape(n, H, C)
            v = (x @ Wv + bv).reshape(n, H, C)
            alpha = jnp.einsum('ehc,ehc->eh', q[dst], k[src]) / jnp.sqrt(jnp.float32(C))
            amax = jax.ops.segment_max(alpha, dst, num_segments=n)
            amax = jax.lax.stop_gradient(jnp.where(jnp.isfinite(amax), amax, 0.0))
            p = jnp.exp(alpha - amax[dst])
            denom = jax.ops.segment_sum(p, dst, num_segments=n) + 1e-16
            out = jax.ops.segment_sum(p[:, :, None] * v[src], dst, num_segments=n)
            out = out / denom[:, :, None]
            out = out.reshape(n, H * C) if concat else out.mean(axis=1)
            return out + x @ Ws + bs
        src, dst = (edge_index[0], edge_index[1])
        h = transformer_conv(x, src, dst, Wq1, bq1, Wk1, bk1, Wv1, bv1, Ws1, bs1, H1, C1, True)
        h = jax.nn.relu(h)
        out = transformer_conv(h, src, dst, Wq2, bq2, Wk2, bk2, Wv2, bv2, Ws2, bs2, H2, C2, False)
        return out

    def _L3_gnn_ref(h, edge_index, ln_gamma, ln_beta, W, b):
        import jax, jax.numpy as jnp
        import numpy as np
        N_NODES = 3125
        N_EDGES = 37500
        IN_DIM = 128
        OUT_DIM = 128
        EPS = 1e-05

        def _layernorm(x, gamma, beta):
            mu = jnp.mean(x, axis=-1, keepdims=True)
            var = jnp.mean(jnp.square(x - mu), axis=-1, keepdims=True)
            return (x - mu) * jax.lax.rsqrt(var + EPS) * gamma + beta
        src, dst = (edge_index[0], edge_index[1])
        n = h.shape[0]
        hn = _layernorm(h, ln_gamma, ln_beta)
        ones = jnp.ones((src.shape[0],), dtype=h.dtype)
        deg_out = jnp.clip(jax.ops.segment_sum(ones, src, num_segments=n), 1.0)
        deg_in = jnp.clip(jax.ops.segment_sum(ones, dst, num_segments=n), 1.0)
        inv_sqrt_out = jax.lax.rsqrt(deg_out)
        inv_sqrt_in = jax.lax.rsqrt(deg_in)
        msg_src = hn * inv_sqrt_out[:, None]
        gathered = msg_src[src]
        agg = jax.ops.segment_sum(gathered, dst, num_segments=n)
        message = agg * inv_sqrt_in[:, None]
        cat = jnp.concatenate([hn, message], axis=1)
        return cat @ W.T + b
    edge_index = jnp.stack([src, dst])
    h = jnp.maximum(_layernorm(x, axis=-1), 0.0)
    x = x + _L0_gnn_ref(h, edge_index, edge_weight, L0_gnn_W0, L0_gnn_b0, L0_gnn_W1, L0_gnn_b1, L0_gnn_fc0, L0_gnn_bf0, L0_gnn_fc1, L0_gnn_bf1)
    h = jnp.maximum(_layernorm(x, axis=-1), 0.0)
    x = x + _L1_gnn_ref(h, edge_index, L1_gnn_W_lin, L1_gnn_b_lin, L1_gnn_W_att, L1_gnn_b_att)
    h = jnp.maximum(_layernorm(x, axis=-1), 0.0)
    x = x + _L2_gnn_ref(h, edge_index, L2_gnn_Wq1, L2_gnn_bq1, L2_gnn_Wk1, L2_gnn_bk1, L2_gnn_Wv1, L2_gnn_bv1, L2_gnn_Ws1, L2_gnn_bs1, L2_gnn_Wq2, L2_gnn_bq2, L2_gnn_Wk2, L2_gnn_bk2, L2_gnn_Wv2, L2_gnn_bv2, L2_gnn_Ws2, L2_gnn_bs2)
    h = jnp.maximum(_layernorm(x, axis=-1), 0.0)
    x = x + _L3_gnn_ref(h, edge_index, L3_gnn_ln_gamma, L3_gnn_ln_beta, L3_gnn_W, L3_gnn_b)
    return x

_drawn_inputs = setup_inputs


def setup_inputs(seed=0):
    import zlib

    import numpy as np

    out = dict(_drawn_inputs(seed))
    spreads = {'L0_gnn_b0': (0.0, 0.1),
     'L0_gnn_b1': (0.0, 0.1),
     'L1_gnn_b_lin': (0.0, 0.1),
     'L1_gnn_b_att': (0.0, 0.8),
     'L3_gnn_ln_gamma': (1.0, 0.2),
     'L3_gnn_ln_beta': (0.0, 0.1),
     'L3_gnn_b': (0.0, 0.1)}
    factors = {'L1_gnn_W_att': 2.844,
     'L2_gnn_Wq1': 43.782,
     'L2_gnn_bq1': 173.056,
     'L2_gnn_Wk1': 44.572,
     'L2_gnn_bk1': 200.0,
     'L2_gnn_bv1': 8.0,
     'L2_gnn_bs1': 8.0,
     'L2_gnn_Wq2': 64.0,
     'L2_gnn_bq2': 200.0,
     'L2_gnn_Wk2': 64.0,
     'L2_gnn_bk2': 200.0,
     'L2_gnn_bv2': 5.102,
     'L2_gnn_bs2': 3.2}
    for name, (base, spread) in spreads.items():
        noise = np.random.default_rng([zlib.crc32(name.encode()), seed]).standard_normal(out[name].shape)
        drawn = base * np.exp(spread * noise) if base else spread * noise
        out[name] = jnp.asarray(drawn.astype(out[name].dtype))
    for name, factor in factors.items():
        out[name] = (out[name] * factor).astype(out[name].dtype)
    return out
```

```python
import concourse.bass as bass
from concourse import mybir
from contextlib import ExitStack

STOP = 1


class Steps:

    def __init__(self, eng, sem, i, per, first=0):
        self.eng, self.sem, self.start, self.per, self.n = eng, sem, i * per + first, per, 0

    def did(self, ins):
        self.n += 1
        ins.then_inc(self.sem, 1)

    def link(self, ins):
        self.did(ins)
        self.eng.wait_ge(self.sem, self.start + self.n)

    def end(self):
        assert self.n == self.per, (self.n, self.per)


def gnn_stack(nc, a, out):
    f32, bf16, i32 = mybir.dt.float32, mybir.dt.bfloat16, mybir.dt.int32
    ALU, ACT, AX = mybir.AluOpType, mybir.ActivationFunctionType, mybir.AxisListType.X
    ds = bass.ds
    x_in, src_in, dst_in, w_in = a["x"], a["src"], a["dst"], a["edge_weight"]

    P, F = 128, 128
    N, E = x_in.shape[0], src_in.shape[0]
    NB = -(-N // P)
    NFULL = N // P
    NREST = N - NFULL * P
    NP = NB * P
    J = 400
    EP = E // J
    U = 16
    HU = U // 2
    G = -(-(E // P + NB) // U)
    T = G * U
    TP = T + 1 + (P * J - E) // P
    KB = NB + 1
    CB = 5
    CH = NB // CB
    CN = CB * P
    BIG = float(2.0 ** 120)
    assert EP * J == E and CH * CB == NB and J % U == 0 and T >= (E + NB * (P - 1)) // P

    ctx = ExitStack()
    with ctx:
        def sb(name, shape, dt=f32):
            return ctx.enter_context(nc.sbuf_tensor(name, shape, dt))

        def sem(name):
            return ctx.enter_context(nc.semaphore(name))

        def dram(name, shape, dt=f32):
            return nc.dram_tensor(name, shape, dt, kind="Internal").ap()

        RW = (4, 3)
        rec_dram = [dram("rec_by_src", [P * TP, RW[0]]), dram("rec_by_dst", [P * TP, RW[1]])]
        relT_dram = [dram("relT_by_src", [T, P], bf16), dram("relT_by_dst", [T, P], bf16)]
        t_v0 = dram("t_v0", [NP, F])
        t_v1 = dram("t_v1", [NP, 65])
        t_sj = dram("t_sj", [NP, 4])
        t_xl = dram("t_xl", [NP, 140])
        t_h2 = dram("t_h2", [NP, F])
        t_k2 = dram("t_k2", [NP, 256])
        t_v2 = dram("t_v2", [NP, 256])
        t_h3 = dram("t_h3", [NP, F])

        x = sb("x_nodes", [P, NB, F])
        acc = sb("acc", [P, NB, 516])
        big = sb("big", [P, NB, 512])
        h2T = sb("h2T", [P, NP])
        rec = [sb("rec_s", [P, T, RW[0]]), sb("rec_d", [P, T, RW[1]])]
        blk = [rec[o][:, :, RW[o] - 1].bitcast(i32) for o in (0, 1)]
        alpha = sb("alpha", [P, T, 4])
        ident = sb("ident", [P, P])
        iota_f = sb("iota_f", [P, P])
        pidx = sb("pidx", [P, 1])
        WORK = 11264
        work = sb("work", [P, WORK])

        def carve(at, shape, dt=f32):
            n = 1
            for s in shape:
                n *= s
            words = n if dt in (f32, i32) else n // 2
            v = work[:, at:at + words]
            if dt != f32:
                v = v.bitcast(dt)
            if len(shape) == 2:
                v = v.rearrange("p (a b) -> p a b", a=shape[0])
            if len(shape) == 3:
                v = v.rearrange("p (a b c) -> p a b c", a=shape[0], b=shape[1])
            return v

        ring = carve(0, [U, 256])
        oh = carve(4096, [U, P])
        ohm = carve(6144, [U, P], bf16)
        wide = carve(7168, [2, 512])
        ohT = carve(8192, [2, HU * P])
        relB = carve(10240, [2, HU * P], bf16)
        hs = carve(0, [CB, F])
        xc = carve(640, [CB, F])
        sq = carve(1280, [CB, F])
        hT = carve(1920, [CN])
        vs = carve(2560, [CB, F])
        st = sb("st", [P, 64])
        idx_slot = sb("idx_slot", [P, U], i32)

        ps = ctx.enter_context(nc.psum_tensor("ps", [P, 8, 512], f32))
        psf = ps[:, :, :].rearrange("p a b -> p (a b)")

        bigf = big[:, :, :].rearrange("p a b -> p (a b)")
        kI, oI = bigf[:, 0:J].bitcast(i32), bigf[:, J:2 * J].bitcast(i32)
        wF = bigf[:, 2 * J:3 * J]
        tI = bigf[:, 3 * J:4 * J].bitcast(i32)
        blkF = bigf[:, 4 * J:5 * J]
        msk, cum, tmp = (bigf[:, n * J:(n + 1) * J] for n in (5, 6, 7))
        zeros = bigf[:, 8 * J:9 * J]
        rank = [bigf[:, 9 * J:10 * J], bigf[:, 10 * J:11 * J]]
        rowI = [bigf[:, n * J:(n + 1) * J].bitcast(i32) for n in (11, 12)]
        recE = [bigf[:, (13 + 4 * o) * J:(13 + 4 * o + RW[o]) * J].rearrange("p (j w) -> p j w", w=RW[o]) for o in (0, 1)]
        tf = bigf[:, 21 * J:22 * J]
        o0 = 22 * J
        relF = bigf[:, o0:o0 + T]
        mapF = bigf[:, o0 + T:o0 + 2 * T]
        iotaT = bigf[:, o0 + 2 * T:o0 + 3 * T]
        relTs = bigf[:, o0 + 3 * T:o0 + 3 * T + 256].bitcast(bf16).rearrange("p (q e) -> p q e", q=4)
        o1 = o0 + 3 * T + 256
        bval = bigf[:, o1:o1 + KB]
        cnt = bigf[:, o1 + 32:o1 + 32 + KB]
        til = bigf[:, o1 + 64:o1 + 64 + KB]
        tilI = bigf[:, o1 + 96:o1 + 96 + KB].bitcast(i32)
        end_ = bigf[:, o1 + 128:o1 + 128 + KB]
        base = bigf[:, o1 + 160:o1 + 160 + KB]
        lower = bigf[:, o1 + 192:o1 + 192 + P]
        ones = bigf[:, o1 + 320:o1 + 320 + P]
        fill = [acc[:, 4 * o:4 * o + 4, :].rearrange("p a b -> p (a b)")[:, 0:TP * RW[o]] for o in (0, 1)]
        assert o1 + 448 + 2 * T <= NB * 512
        sc_idx = sb("sc_idx", [P, U], i32)
        sc_rec = [sb("sc_rec_s", [P, U, RW[0]]), sb("sc_rec_d", [P, U, RW[1]])]
        mapI = [bigf[:, o1 + 448 + o * T:o1 + 448 + (o + 1) * T].bitcast(i32) for o in (0, 1)]
        TQ = T // 4

        node1 = sb("node1", [P, NB, 16])
        mx = sb("mx", [P, NB, 4])
        sums = sb("sums", [P, NB, 5])
        tmN = sb("tmN", [P, NB])
        stb = sb("stb", [P, 2 * CB, 4])
        deg_in = sb("deg_in", [P, NB])
        pE = sb("pE", [P, 2, HU, 5])
        zE = sb("zE", [P, 2, HU, 4])
        aS = sb("aS", [P, U, 4])
        tm = sb("tm", [P, 4, 4])
        ident_b = sb("ident_b", [P, P], bf16)
        xl = bigf[:, 0:NP].rearrange("p (b f) -> p b f", f=F)
        q2 = bigf[:, 0:2 * NP].rearrange("p (b f) -> p b f", f=256)
        s2 = bigf[:, 2 * NP:3 * NP].rearrange("p (b f) -> p b f", f=F)
        kv = bigf[:, 3 * NP:3 * NP + CB * 512].rearrange("p (b f) -> p b f", f=512)
        xlT = carve(3200, [CN])
        qT = carve(3840, [2, CN])
        aT = carve(0, [4, CN])
        h1T = carve(2560, [4, CN])
        flT = carve(5120, [CN])
        wl2 = carve(5760, [4, 896])
        bl2 = carve(9344, [896])
        an = h1T.rearrange("p a b -> p (a b)").rearrange("p (b h c) -> p b h c", b=CB, h=4)

        wlin = h2T[:, 384:512]
        watt = sb("watt", [P, 8])
        blinT = sb("blinT", [P, 1])
        battb = sb("battb", [P, 4])
        wq1 = sb("wq1", [P, 512])
        wk1 = carve(5120, [512])
        wv1 = sb("wv1", [P, 512])
        ws1 = sb("ws1", [P, 512])
        wkT = sb("wkT", [P, 4, 129])
        bq1T = sb("bq1T", [P, 4])
        bs1T = sb("bs1T", [P, 4])
        bv4 = sb("bv4", [4, 4, 128])
        w3 = carve(5632, [256])
        w3T = sb("w3T", [P, 2, 128])
        rows3 = sb("rows3", [P, 4, 128])
        w01 = h2T[:, 0:128]
        brow = h2T[:, 128:384].rearrange("p (a b) -> p a b", a=2)
        bf_b = sb("bf_b", [P, 2])

        s_cst = sem("constants_ready")
        s_x = sem("x_loaded")
        s_xz = sem("x_zeroed")
        s_key = sem("edges_loaded")
        s_w0 = sem("weights0_loaded")
        s_pad = sem("pads_set")
        s_filled = sem("rec_dram_filled")
        v_s = [sem("sort_dve_s"), sem("sort_dve_d")]
        s_pref = sem("prefix")
        s_pos = sem("rows_ready")
        s_cp = sem("scatter_slots_filled")
        s_sc = [sem("scatter_half0"), sem("scatter_half1")]
        s_scd = sem("scatter_order_done")
        s_gate = sem("pool_gate")
        s_rec = sem("rec_back")
        s_relf = sem("rel_compact")
        s_relp = sem("rel_transposed")
        s_rele = sem("rel_evac")
        s_relw = sem("rel_written")
        s_gath = [sem(f"gathered{k}") for k in range(U)]
        s_out = sem("out_written")
        s_wt = sem("weights_loaded")
        s_wT = sem("weights_transposed")
        s_wTe = sem("weights_transposed_copied")
        NWT = 28

        block = ctx.enter_context(nc.Block())

        NLN = 9
        VAR = 6
        PRE = 7

        def table_rows(t, i):
            return t[ds(i * CN, CN), :].rearrange("(b p) f -> p b f", p=P)

        made = {}

        def ph(name):
            if name not in made:
                made[name] = sem(name)
            return made[name]

        EARLIER = {"L0h2": ("L0h1", 1), "L3": ("L0h1", 2), "L2D": ("L2A", 1), "L2F": ("L2C", 1)}

        def sig(name, what):
            return ph(EARLIER.get(name, (name, 0))[0] + what)

        def nth(name, i):
            return i + EARLIER.get(name, (name, 0))[1] * G

        def credit(eng, name, what, n):
            if name not in EARLIER:
                eng.sem_inc(sig(name, what), n)

        def all_added(name):
            return nth(name, G) * U + U

        rounds = {n: r for r, n in enumerate(("L0h1", "L0h2", "L1A", "L1C", "L2A", "L2C", "L2D", "L2F", "L3"))}
        rel_rounds = {n: r for r, n in enumerate(("L1B", "L1C", "L2A", "L2C", "L2D", "L2F"))}
        heads = {"L1A": 4, "L2A": 4, "L2C": 4, "L2D": 2, "L2F": 2}
        s_relB = [sem("rel_rows0"), sem("rel_rows1")]
        ROOTD = float(F) ** -0.5

        @block.sync
        def _(sp):
            sp.wait_ge(s_pad, 1)
            sp.dma_start(kI[0:EP, :], src_in.rearrange("(p j) -> p j", j=J)).then_inc(s_key, 16)
            sp.dma_start(oI[0:EP, :], dst_in.rearrange("(p j) -> p j", j=J)).then_inc(s_key, 16)
            sp.dma_start(wF[0:EP, :], w_in.rearrange("(p j) -> p j", j=J)).then_inc(s_key, 16)
            sp.wait_ge(s_xz, 1)
            sp.dma_start(x[:, 0:NFULL, :], x_in[0:NFULL * P, :].rearrange("(b p) f -> p b f", p=P)).then_inc(s_x, 16)
            sp.dma_start(x[0:NREST, NFULL, :], x_in[NFULL * P:N, :]).then_inc(s_x, 16)
            sp.dma_start(w01[:, 0:64], a["L0_gnn_W0"]).then_inc(s_w0, 16)
            sp.dma_start(w01[:, 64:128], a["L0_gnn_W1"]).then_inc(s_w0, 16)
            for n, nm in enumerate(("b0", "b1", "fc0", "fc1")):
                v = a["L0_gnn_" + nm]
                v = v if n < 2 else v.rearrange("a b -> (a b)")
                sp.dma_start(brow[:, n // 2, (n % 2) * 64:(n % 2) * 64 + 64], v.partition_broadcast(P)).then_inc(s_w0, 16)
            for n in (0, 1):
                sp.dma_start(bf_b[:, n:n + 1], a[f"L0_gnn_bf{n}"].partition_broadcast(P)).then_inc(s_w0, 16)
            wts = [(wlin[:, :], a["L1_gnn_W_lin"]),
                   (watt[:, 0:4], a["L1_gnn_W_att"][0:F, :]), (watt[:, 4:8], a["L1_gnn_W_att"][F:2 * F, :]),
                   (blinT[:, :], a["L1_gnn_b_lin"].rearrange("(f a) -> f a", a=1)),
                   (battb[:, :], a["L1_gnn_b_att"].partition_broadcast(P)),
                   (wq1[:, :], a["L2_gnn_Wq1"]), (wv1[:, :], a["L2_gnn_Wv1"]), (ws1[:, :], a["L2_gnn_Ws1"]),
                   (rows3[:, 0, :], a["L3_gnn_ln_gamma"].partition_broadcast(P)),
                   (rows3[:, 1, :], a["L3_gnn_ln_beta"].partition_broadcast(P)),
                   (rows3[:, 2, :], a["L3_gnn_b"].partition_broadcast(P)),
                   (rows3[:, 3, :], a["L1_gnn_b_lin"].partition_broadcast(P))]
            for h in range(4):
                wts.append((wkT[:, h, 128:129], a["L2_gnn_bk1"][h * F:(h + 1) * F].rearrange("(f a) -> f a", a=1)))
                wts.append((bq1T[:, h:h + 1], a["L2_gnn_bq1"][h * F:(h + 1) * F].rearrange("(f a) -> f a", a=1)))
                wts.append((bs1T[:, h:h + 1], a["L2_gnn_bs1"][h * F:(h + 1) * F].rearrange("(f a) -> f a", a=1)))
                wts.append((bv4[h:h + 1, h, :], a["L2_gnn_bv1"][h * F:(h + 1) * F].rearrange("(a f) -> a f", a=1)))
            assert len(wts) == NWT
            for dst_t, w in wts:
                sp.dma_start(dst_t, w).then_inc(s_wt, 16)
            for o in (0, 1):
                sp.wait_ge(s_pad, 1)
                sp.dma_start(rec_dram[o].rearrange("(p t) w -> p (t w)", p=P), fill[o]).then_inc(s_filled, 16)
            with sp.Fori(0, CH) as i:
                sp.wait_ge(ph("n0_evac"), i + 2)
                sp.dma_start(table_rows(t_v0, i), vs).then_inc(ph("n0_table"), 16)
                sp.wait_ge(ph("n0_table"), i * 16 + 16)
                sp.sem_inc(ph("n0_stored"), 1)

            def records_back(o):
                sp.wait_ge(s_scd, o + 1)
                sp.dma_start(rec[o][:, :, :].rearrange("p t w -> p (t w)"),
                             rec_dram[o].rearrange("(p t) w -> p (t w)", p=P)[:, 0:T * RW[o]]).then_inc(s_rec, 16)

            def rel_rows_out(o):
                sp.wait_ge(s_rele, (o + 1))
                sp.dma_start(relT_dram[o].rearrange("(q r) e -> r q e", q=4), relTs[0:TQ, :, :]).then_inc(s_relw, 16)

            records_back(0)
            rel_rows_out(0)
            records_back(1)
            sp.wait_ge(sig("L0h1", "_added"), all_added("L0h1"))
            sp.dma_start(t_v1.rearrange("(b p) f -> p b f", p=P), acc[:, :, 64:129]).then_inc(ph("v1_table"), 16)
            rel_rows_out(1)
            def rel_rows(name, o):
                credit(sp, name, "_ohT", 2)
                with sp.Fori(0, G) as i:
                    for h in (0, 1):
                        sp.wait_ge(sig(name, "_ohT"), nth(name, i) * 2 + h + 1)
                        rows = relT_dram[o][ds(i * U + h * HU, HU), :].rearrange("t e -> (t e)")
                        sp.dma_start(relB[:, h, :], rows.partition_broadcast(P)).then_inc(s_relB[h], 16)

            def node_table(name, table, tile, ready_offset=0):
                with sp.Fori(0, CH) as i:
                    sp.wait_ge(sig(name, "_filled"), i + 1)
                    sp.dma_start(table_rows(table, i), tile).then_inc(sig(name, "_table"), 16)
                    sp.wait_ge(sig(name, "_table"), nth(name, i) * 16 + 16)
                    credit(sp, name, "_stored", 1)

            sp.wait_ge(ph("n1_done"), 1)
            sp.dma_start(t_sj.rearrange("(b p) f -> p b f", p=P), node1[:, :, 12:16]).then_inc(ph("sj_table"), 16)
            sp.dma_start(t_xl.rearrange("(b p) f -> p b f", p=P)[:, :, 0:F], xl).then_inc(ph("xl_table"), 16)
            sp.wait_ge(sig("L1A", "_added"), all_added("L1A"))
            rel_rows("L1B", 0)
            sp.wait_ge(ph("n1_sums"), 1)
            sp.dma_start(t_xl.rearrange("(b p) f -> p b f", p=P)[:, :, F:F + 12], node1[:, :, 0:12]).then_inc(ph("xl_table"), 16)
            rel_rows("L1C", 1)
            sp.wait_ge(sig("L1C", "_added"), all_added("L1C"))
            sp.dma_start(wk1, a["L2_gnn_Wk1"]).then_inc(ph("wraw"), 16)
            sp.dma_start(w3, a["L3_gnn_W"]).then_inc(ph("wraw"), 16)
            node_table("n2", t_h2, hs)
            rel_rows("L2A", 1)
            sp.wait_ge(sig("L2A", "_added"), all_added("L2A"))
            rel_rows("L2C", 1)
            sp.wait_ge(sig("L2C", "_added"), all_added("L2C"))
            for n, (c, nm) in enumerate(((0, "q"), (256, "k"), (512, "v"), (768, "s"))):
                w = 128 if nm == "s" else 256
                sp.dma_start(wl2[:, :, c:c + w], a[f"L2_gnn_W{nm}2"].rearrange("(h p) f -> p h f", p=P)).then_inc(ph("wl2"), 16)
                sp.dma_start(bl2[:, c:c + w], a[f"L2_gnn_b{nm}2"].partition_broadcast(P)).then_inc(ph("wl2"), 16)
            with sp.Fori(0, CH) as i:
                sp.wait_ge(ph("n2b_filled"), i + 1)
                sp.dma_start(table_rows(t_k2, i), kv[:, :, 0:256]).then_inc(ph("n2b_table"), 16)
                sp.dma_start(table_rows(t_v2, i), kv[:, :, 256:512]).then_inc(ph("n2b_table"), 16)
                sp.wait_ge(ph("n2b_table"), i * 32 + 32)
                sp.sem_inc(ph("n2b_stored"), 1)
            rel_rows("L2D", 1)
            sp.wait_ge(sig("L2D", "_added"), all_added("L2D"))
            rel_rows("L2F", 1)
            node_table("n3", t_h3, vs)
            sp.wait_ge(ph("final"), 1)
            sp.dma_start(out[0:NFULL * P, :].rearrange("(b p) f -> p b f", p=P), x[:, 0:NFULL, :]).then_inc(s_out, 16)
            sp.dma_start(out[NFULL * P:N, :], x[0:NREST, NFULL, :]).then_inc(s_out, 16)
            sp.wait_ge(s_out, 32)
            for o in (0, 1):
                sp.wait_ge(s_relw, (o + 1) * 16)

        @block.gpsimd
        def _(pool):
            nc.gpsimd.memset(ident[:, :], 0.0).then_inc(s_cst, 1)
            nc.gpsimd.memset(lower, 1.0).then_inc(s_cst, 1)
            nc.gpsimd.iota(iota_f[:, :], [[1, P]], base=0, channel_multiplier=0, allow_small_or_imprecise_dtypes=True).then_inc(s_cst, 1)
            nc.gpsimd.iota(pidx[:, :], [[0, 1]], base=0, channel_multiplier=1, allow_small_or_imprecise_dtypes=True).then_inc(s_cst, 1)
            nc.gpsimd.iota(bval, [[1, KB]], base=0, channel_multiplier=0, allow_small_or_imprecise_dtypes=True).then_inc(s_cst, 1)
            nc.gpsimd.iota(iotaT, [[1, T]], base=0, channel_multiplier=0, allow_small_or_imprecise_dtypes=True).then_inc(s_cst, 1)
            nc.gpsimd.memset(ones, 1.0).then_inc(s_cst, 1)
            pool.wait_ge(s_cst, 7)
            nc.gpsimd.affine_select(out=ident[:, :], in_=ident[:, :], compare_op=ALU.not_equal, fill=1.0,
                                    base=0, pattern=[[-1, P]], channel_multiplier=1).then_inc(s_cst, 1)
            nc.gpsimd.affine_select(out=lower, in_=lower, compare_op=ALU.is_gt, fill=0.0,
                                    base=0, pattern=[[1, P]], channel_multiplier=-1).then_inc(s_cst, 1)

            def scatter(o):
                pool.wait_ge(s_pos, (o + 1))
                pool.sem_inc(s_gate, 1)
                pool.wait_ge(s_filled, 32)
                pool.sem_inc(s_gate, 1)
                SG = J // U

                def body(i, first):
                    for h in (0, 1):
                        j = i * U + h * HU
                        if not first:
                            pool.wait_ge(s_sc[h], (i + o * SG) * HU * 16)
                            pool.sem_inc(s_gate, 1)
                        nc.gpsimd.tensor_copy(sc_idx[:, h * HU:(h + 1) * HU], rowI[o][:, ds(j, HU)]).then_inc(s_cp, 1)
                        nc.gpsimd.tensor_copy(sc_rec[o][:, h * HU:(h + 1) * HU, :], recE[o][:, ds(j, HU), :]).then_inc(s_cp, 1)
                        pool.wait_ge(s_cp, (i + o * SG) * 4 + 2 * h + 2)
                        pool.sem_inc(s_gate, 1)
                        for k in range(h * HU, (h + 1) * HU):
                            nc.gpsimd.indirect_dma_start(
                                rec_dram[o], bass.IndirectOffsetOnAxis(ap=sc_idx[:, k:k + 1], axis=0),
                                sc_rec[o][:, k, :], None).then_inc(s_sc[h], 16)

                body(0, o == 0)
                with pool.Fori(1, SG) as i:
                    body(i, False)
                for h in (0, 1):
                    pool.wait_ge(s_sc[h], (o + 1) * SG * HU * 16)
                pool.sem_inc(s_scd, 1)

            def gathers(name, o, table, width):
                col = ring
                credit(pool, name, "_added", U)
                with pool.Fori(0, G) as i:
                    for h in (0, 1):
                        pool.wait_ge(sig(name, "_added"), nth(name, i) * U + (h + 1) * HU)
                        pool.sem_inc(s_gate, 1)
                        nc.gpsimd.tensor_copy(idx_slot[:, h * HU:(h + 1) * HU],
                                              rec[o][:, ds(i * U + h * HU, HU), 0].bitcast(i32)).then_inc(sig(name, "_idx"), 1)
                        pool.wait_ge(sig(name, "_idx"), nth(name, i) * 2 + h + 1)
                        pool.sem_inc(s_gate, 1)
                        for k in range(h * HU, (h + 1) * HU):
                            nc.gpsimd.indirect_dma_start(
                                col[:, k, 0:width], None, table,
                                bass.IndirectOffsetOnAxis(ap=idx_slot[:, k:k + 1], axis=0)).then_inc(s_gath[k], 16)

            scatter(0)
            pool.wait_ge(s_rec, 16)
            pool.sem_inc(s_gate, 1)
            pool.wait_ge(ph("n0_table"), CH * 16)
            pool.sem_inc(s_gate, 1)
            gathers("L0h1", 0, t_v0, 128)
            scatter(1)
            pool.wait_ge(ph("v1_table"), 16)
            pool.sem_inc(s_gate, 1)
            gathers("L0h2", 0, t_v1, 65)

            def table_ready(name, count):
                pool.wait_ge(ph(name), count)
                pool.sem_inc(s_gate, 1)

            table_ready("sj_table", 16)
            gathers("L1A", 0, t_sj, 4)
            table_ready("xl_table", 32)
            gathers("L1C", 1, t_xl, 140)
            table_ready("n2_table", 16 * CH)
            table_ready("n2_free", 1)
            gathers("L2A", 1, t_h2, F)
            pool.wait_ge(sig("L2A", "_added"), all_added("L2A"))
            pool.sem_inc(s_gate, 1)
            gathers("L2C", 1, t_h2, F)
            table_ready("n2b_table", 32 * CH)
            table_ready("n2b_free", 1)
            gathers("L2D", 1, t_k2, 256)
            pool.wait_ge(sig("L2D", "_added"), all_added("L2D"))
            pool.sem_inc(s_gate, 1)
            gathers("L2F", 1, t_v2, 256)
            table_ready("n3_table", 16 * CH)
            table_ready("n3_free", 1)
            gathers("L3", 1, t_h3, F)

        @block.vector
        def _(dve):
            V = nc.vector
            V.memset(kI, NP).then_inc(v_s[0], 1)
            V.memset(oI, NP).then_inc(v_s[0], 1)
            V.memset(wF, 0.0).then_inc(v_s[0], 1)
            V.memset(zeros, 0.0).then_inc(v_s[0], 1)
            V.memset(acc[:, 0:8, :].rearrange("p a b -> p (a b)"), 0.0).then_inc(v_s[0], 1)
            dve.wait_ge(v_s[0], 5)
            V.memset(bv4[:, :, :], 0.0)
            V.memset(fill[0].rearrange("p (t w) -> p t w", w=RW[0])[:, :, 1], -1.0)
            V.memset(fill[1].rearrange("p (t w) -> p t w", w=RW[1])[:, :, 1], -1.0).then_inc(s_pad, 1)
            V.memset(x[:, NFULL, :], 0.0).then_inc(s_xz, 1)
            V.memset(recE[0].rearrange("p j w -> p (j w)"), 0.0).then_inc(v_s[0], 1)
            V.memset(recE[1].rearrange("p j w -> p (j w)"), 0.0).then_inc(v_s[0], 1)

            def bucket(o, first):
                key, other = (kI, oI) if o == 0 else (oI, kI)
                s = Steps(dve, v_s[o], 0, 0, first)
                s.link(V.tensor_single_scalar(tI, key, 7, ALU.arith_shift_right))
                s.link(V.tensor_copy(blkF, tI))
                s.link(V.tensor_single_scalar(tI, key, P - 1, ALU.bitwise_and))
                s.link(V.tensor_copy(recE[o][:, :, 1], tI))
                s.link(V.tensor_copy(recE[o][:, :, 0].bitcast(i32), other))
                s.link(V.tensor_copy(recE[0][:, :, 2], wF) if o == 0 else V.memset(tmp, 0.0))
                s.link(V.memset(rank[o], 0.0))
                s.link(V.memset(mapF, 0.0))
                with dve.Fori(0, KB) as b:
                    l = Steps(dve, v_s[o], b, 5, s.start + s.n)
                    l.link(V.tensor_scalar(msk, blkF, bval[:, ds(b, 1)], None, ALU.is_equal))
                    l.link(V.tensor_tensor_scan(cum, msk, zeros, 0.0, ALU.add, ALU.max))
                    l.link(V.tensor_copy(cnt[:, ds(b, 1)], cum[:, J - 1:J]))
                    l.link(V.tensor_tensor(tmp, msk, cum, ALU.mult))
                    l.link(V.tensor_tensor(rank[o], rank[o], tmp, ALU.add))
                    l.end()
                s.n += KB * 5
                dve.wait_ge(s_pref, (o + 1))
                s.link(V.tensor_scalar(tilI, ps[:, 7, 0:KB], float(P - 1), None, ALU.add))
                s.link(V.tensor_single_scalar(tilI, tilI, 7, ALU.arith_shift_right))
                s.link(V.tensor_copy(til, tilI))
                s.link(V.tensor_tensor_scan(end_, til, zeros[:, 0:KB], 0.0, ALU.add, ALU.max))
                s.link(V.tensor_tensor(base, end_, til, ALU.subtract))
                s.link(V.memset(base[:, NB:KB], float(T)))
                s.link(V.tensor_scalar(base, base, float(P), -1.0, ALU.mult, ALU.add))
                s.link(V.tensor_tensor(base, base, ps[:, 6, 0:KB], ALU.add))
                with dve.Fori(0, KB) as b:
                    l = Steps(dve, v_s[o], b, 3, s.start + s.n)
                    l.link(V.tensor_scalar(tmp, blkF, bval[:, ds(b, 1)], base[:, ds(b, 1)], ALU.is_equal, ALU.mult))
                    l.link(V.tensor_tensor(rank[o], rank[o], tmp, ALU.add))
                    l.link(V.scalar_tensor_tensor(mapF, iotaT, end_[:, ds(b, 1)], mapF, ALU.is_ge, ALU.add))
                    l.end()
                s.n += KB * 3
                s.link(V.tensor_scalar(mapI[o], mapF, float(NB - 1), None, ALU.min))
                s.link(V.tensor_copy(tI, rank[o]))
                s.link(V.tensor_single_scalar(rowI[o], tI, P - 1, ALU.bitwise_and))
                s.link(V.tensor_copy(tmp, rowI[o]))
                s.link(V.tensor_single_scalar(tI, tI, 7, ALU.arith_shift_right))
                s.link(V.tensor_copy(tf, tI))
                V.scalar_tensor_tensor(rowI[o], tmp, float(TP), tf, ALU.mult, ALU.add).then_inc(s_pos, 1)
                dve.wait_ge(s_pos, (o + 1))
                return s.n

            def layer_norm(s, xin, root_ready):
                s.link(V.tensor_reduce(st[:, 0:CB], xin, AX, ALU.add))
                s.link(V.tensor_scalar(st[:, 8:8 + CB], st[:, 0:CB], 1.0 / F, None, ALU.mult))
                s.link(V.tensor_tensor(xc, xin, st[:, 8:8 + CB].unsqueeze(2).to_broadcast([P, CB, F]), ALU.subtract))
                s.link(V.tensor_tensor(sq, xc, xc, ALU.mult))
                s.link(V.tensor_reduce(st[:, 16:16 + CB], sq, AX, ALU.add))
                s.link(V.tensor_scalar(st[:, 24:24 + CB], st[:, 16:16 + CB], 1.0 / F, 1e-5, ALU.mult, ALU.add))
                root_ready()
                s.link(V.reciprocal(st[:, 40:40 + CB], st[:, 32:32 + CB]))
                s.link(V.tensor_tensor(hs, xc, st[:, 40:40 + CB].unsqueeze(2).to_broadcast([P, CB, F]), ALU.mult))

            def sweep_weighted(name, o, width, at, weighted):
                with dve.Fori(0, G) as i:
                    for h in (0, 1):
                        for k in range(h * HU, (h + 1) * HU):
                            t = i * U + k
                            dve.wait_ge(sig(name, "_product"), nth(name, i) * U + k + 1)
                            if weighted:
                                V.tensor_scalar(oh[:, k, :], iota_f[:, :], rec[o][:, ds(t, 1), 1], rec[o][:, ds(t, 1), 2],
                                                ALU.is_equal, ALU.mult).then_inc(sig(name, "_onehot"), 1)
                            else:
                                V.tensor_scalar(oh[:, k, :], iota_f[:, :], rec[o][:, ds(t, 1), 1], None,
                                                ALU.is_equal).then_inc(sig(name, "_onehot"), 1)
                        for k in range(h * HU, (h + 1) * HU):
                            b = dve.value_load(blk[o][0:1, ds(i * U + k, 1)], min_val=0, max_val=NB - 1)
                            dve.wait_ge(sig(name, "_product"), nth(name, i) * U + U + k + 1)
                            dve.wait_ge(sig(name, "_added"), nth(name, i) * U + U + k)
                            part = acc[:, ds(b, 1), at:at + width]
                            V.tensor_tensor(part, part, ps[:, k % 8, 0:width].unsqueeze(1), ALU.add).then_inc(sig(name, "_added"), 1)

            dve.wait_ge(s_key, 48)
            dve.wait_ge(s_cst, 9)
            dve.wait_ge(v_s[0], PRE)
            done = bucket(0, PRE)

            dve.wait_ge(s_x, 32)
            PER = NLN
            dve.sem_inc(ph("n0_transposed"), 1)
            with dve.Fori(0, CH) as i:
                s = Steps(dve, ph("n0_dve"), i, PER)
                dve.wait_ge(ph("n0_transposed"), i + 1)
                layer_norm(s, x[:, ds(i * CB, CB), :], lambda: dve.wait_ge(ph("n0_root"), i + 1))
                s.link(V.tensor_scalar(hs, hs, 0.0, None, ALU.max))
                s.end()
            bucket(1, 0)

            dve.wait_ge(s_rec, 16)
            V.tensor_copy(blk[0], mapI[0]).then_inc(s_relf, 1)
            V.tensor_copy(relF, rec[0][:, :, 1]).then_inc(s_relf, 1)
            dve.wait_ge(s_relf, 2)
            dve.wait_ge(ph("n0_table"), 16 * CH)
            V.memset(ring[:, :, 128:129], 1.0).then_inc(ph("L0_ones"), 1)
            V.memset(acc[:, :, :].rearrange("p a b -> p (a b)"), 0.0).then_inc(ph("L0_zero"), 1)
            dve.wait_ge(ph("L0_zero"), 1)
            sweep_weighted("L0h1", 0, 129, 0, True)
            dve.wait_ge(s_rec, 32)
            dve.wait_ge(s_rele, 1)
            V.tensor_copy(blk[1], mapI[1]).then_inc(s_relf, 1)
            V.tensor_copy(relF, rec[1][:, :, 1]).then_inc(s_relf, 1)
            dve.wait_ge(s_relf, 4)
            dve.wait_ge(sig("L0h1", "_added"), all_added("L0h1"))
            sweep_weighted("L0h2", 0, 65, 129, True)
            dve.wait_ge(sig("L0h2", "_added"), all_added("L0h2"))

            dve.wait_ge(s_w0, 128)
            NE = 15
            with dve.Fori(0, CH) as i:
                for hop in (0, 1):
                    s = Steps(dve, ph("l0e_dve"), i, 2 * NE)
                    s.n = hop * NE
                    c0, dc = ((0, 128), (129, 193))[hop]
                    part = ds(i * CB, CB)
                    deg = acc[:, part, dc]
                    m, t, r = st[:, 0:CB], st[:, 8:8 + CB], st[:, 16:16 + CB]
                    z, g = st[:, 24:24 + CB], st[:, 32:32 + CB]
                    y, q, n = hs[:, :, 0:64], xc[:, :, 0:64], sq[:, :, 0:64]
                    s.link(V.tensor_scalar(m, deg, 0.0, None, ALU.is_gt))
                    s.link(V.tensor_tensor(t, deg, m, ALU.mult))
                    s.link(V.tensor_scalar(r, m, -1.0, 1.0, ALU.mult, ALU.add))
                    s.link(V.tensor_tensor(t, t, r, ALU.add))
                    s.link(V.reciprocal(r, t))
                    s.link(V.tensor_tensor(r, r, m, ALU.mult))
                    s.link(V.tensor_tensor(y, acc[:, part, c0:c0 + 64], r.unsqueeze(2).to_broadcast([P, CB, 64]), ALU.mult))
                    s.link(V.tensor_tensor(y, y, brow[:, 0:1, hop * 64:hop * 64 + 64].to_broadcast([P, CB, 64]), ALU.add))
                    s.link(V.tensor_tensor(q, y, brow[:, 1:2, hop * 64:hop * 64 + 64].to_broadcast([P, CB, 64]), ALU.mult))
                    s.link(V.tensor_reduce(z, q, AX, ALU.add))
                    s.link(V.tensor_scalar(n, y, 0.0, None, ALU.min))
                    dve.wait_ge(ph("l0e_gate"), i * 2 + hop + 1)
                    s.link(V.tensor_tensor(n, n, g.unsqueeze(2).to_broadcast([P, CB, 64]), ALU.mult))
                    s.link(V.tensor_scalar(y, y, 0.0, None, ALU.max))
                    s.link(V.tensor_tensor(y, y, n, ALU.add))
                    xp = x[:, part, hop * 64:hop * 64 + 64]
                    s.link(V.tensor_tensor(xp, xp, y, ALU.add))
            def bc(v, n):
                return v.unsqueeze(len(v.shape)).to_broadcast(list(v.shape) + [n])

            def node_block(o, i, k):
                return dve.value_load(blk[o][0:1, ds(i * U + k, 1)], min_val=0, max_val=NB - 1)

            def halves(name, o, i, h):
                dve.wait_ge(s_relB[h], (i + rel_rounds[name] * G) * 16 + 16)
                dve.wait_ge(sig(name, "_looked"), nth(name, i) * U + (h + 1) * HU)
                V.tensor_scalar(ohT[:, h, :], relB[:, h, :], pidx[:, 0:1], None, ALU.is_equal).then_inc(sig(name, "_ohT"), 1)

            def one_hot(name, o, i, k, mask=False):
                dve.wait_ge(sig(name, "_product"), nth(name, i) * U + k + 1)
                ins = V.tensor_scalar(oh[:, k, :], iota_f[:, :], rec[o][:, ds(i * U + k, 1), 1], None, ALU.is_equal)
                if mask:
                    ins = V.tensor_scalar(ohm[:, k, :], iota_f[:, :], rec[o][:, ds(i * U + k, 1), 1], -BIG,
                                          ALU.not_equal, ALU.mult)
                ins.then_inc(sig(name, "_onehot"), 1)

            def take_max(name, o, i, k):
                H = heads[name]
                b = node_block(o, i, k)
                dve.wait_ge(sig(name, "_product"), nth(name, i) * U + U + k + 1)
                V.tensor_reduce(tm[:, k % 4, 0:H], ps[:, 2 + k % 4, 0:H * P].rearrange("p (h e) -> p h e", h=H), AX,
                                ALU.max).then_inc(sig(name, "_reduced"), 1)
                dve.wait_ge(sig(name, "_reduced"), nth(name, i) * U + k + 1)
                dve.wait_ge(sig(name, "_added"), nth(name, i) * U + U + k)
                part = mx[:, ds(b, 1), 0:H]
                V.tensor_tensor(part, part, tm[:, k % 4, 0:H].unsqueeze(1), ALU.max).then_inc(sig(name, "_added"), 1)

            flow = Steps(dve, ph("flow"), 0, 0)
            link = flow.link

            link(V.tensor_copy(ident_b[:, :], ident[:, :]))
            dve.wait_ge(s_relw, 32)
            dve.wait_ge(s_wt, NWT * 16)
            dve.sem_inc(ph("n1_transposed"), 1)
            N1 = NLN + 3
            with dve.Fori(0, CH) as i:
                s = Steps(dve, ph("n1_dve"), i, N1)
                dve.wait_ge(ph("n1_transposed"), i + 1)
                layer_norm(s, x[:, ds(i * CB, CB), :], lambda: dve.wait_ge(ph("n1_root"), i + 1))
                s.link(V.tensor_scalar(hs, hs, 0.0, None, ALU.max))
                dve.wait_ge(ph("n1_mm"), i + 1)
                s.link(V.tensor_tensor(xl[:, ds(i * CB, CB), :], psf[:, 1024:1024 + CN].rearrange("p (b f) -> p b f", f=F),
                                       rows3[:, 3:4, :].to_broadcast([P, CB, F]), ALU.add))
                dve.wait_ge(ph("n1_att"), i + 1)
                pa = psf[:, 3072:3072 + CB * 8].rearrange("p (b f) -> p b f", f=8)
                s.link(V.tensor_tensor(node1[:, ds(i * CB, CB), 0:4], pa[:, :, 0:4],
                                       battb[:, :].unsqueeze(1).to_broadcast([P, CB, 4]), ALU.add))
                s.link(V.tensor_copy(node1[:, ds(i * CB, CB), 12:16], pa[:, :, 4:8]))
                s.end()
            link(V.memset(mx[:, :, :], -1e30))
            link(V.memset(sums[:, :, :], 0.0))
            V.memset(pE[:, :, :, :], 1.0).then_inc(ph("n1_done"), 1)
            dve.wait_ge(ph("n1_done"), 1)

            def sweep_max(name, o):
                with dve.Fori(0, G) as i:
                    for h in (0, 1):
                        for k in range(h * HU, (h + 1) * HU):
                            one_hot(name, o, i, k, True)
                        for k in range(h * HU, (h + 1) * HU):
                            take_max(name, o, i, k)

            sweep_max("L1A", 0)
            dve.wait_ge(sig("L1A", "_added"), all_added("L1A"))
            link(V.tensor_tensor(node1[:, :, 4:8], node1[:, :, 0:4], mx[:, :, :], ALU.add))
            link(V.scalar_tensor_tensor(node1[:, :, 4:8], node1[:, :, 4:8], 0.2, node1[:, :, 4:8], ALU.mult, ALU.max))

            with dve.Fori(0, G) as i:
                for h in (0, 1):
                    halves("L1B", 0, i, h)
                    for k in range(h * HU, (h + 1) * HU):
                        one_hot("L1B", 0, i, k)
                    s = Steps(dve, ph("L1B_dve"), i, 6)
                    s.n = 3 * h
                    dve.wait_ge(ph("L1B_looked"), i * U + U + (h + 1) * HU)
                    pl = ps[:, h, 0:64].rearrange("p (k f) -> p k f", f=8)
                    z = zE[:, h, :, :]
                    s.link(V.tensor_tensor(z, alpha[:, ds(i * U + h * HU, HU), :], pl[:, :, 0:4], ALU.add))
                    s.link(V.scalar_tensor_tensor(z, z, 0.2, z, ALU.mult, ALU.max))
                    s.link(V.tensor_tensor(z, z, pl[:, :, 4:8], ALU.subtract))
                    dve.wait_ge(ph("L1B_product"), i * U + U + (h + 1) * HU)
                    for k in range(h * HU, (h + 1) * HU):
                        b = node_block(0, i, k)
                        dve.wait_ge(ph("L1B_added"), i * U + U + k)
                        part = sums[:, ds(b, 1), :]
                        V.tensor_tensor(part, part, ps[:, 2 + h, (k % HU) * 8:(k % HU) * 8 + 5].unsqueeze(1), ALU.add)\
                            .then_inc(ph("L1B_added"), 1)
            dve.wait_ge(ph("L1B_added"), T + U)
            link(V.tensor_scalar(node1[:, :, 8:12], sums[:, :, 0:4], 1e-16, None, ALU.add))
            V.reciprocal(node1[:, :, 8:12], node1[:, :, 8:12]).then_inc(ph("n1_sums"), 1)
            link(V.memset(acc[:, :, :].rearrange("p a b -> p (a b)"), 0.0))
            dve.wait_ge(ph("n1_sums"), 1)

            with dve.Fori(0, G) as i:
                for h in (0, 1):
                    halves("L1C", 1, i, h)
                    for k in range(h * HU, (h + 1) * HU):
                        one_hot("L1C", 1, i, k)
                    s = Steps(dve, ph("L1C_dve"), i, 12)
                    s.n = 6 * h
                    dve.wait_ge(ph("L1C_looked"), i * U + U + (h + 1) * HU)
                    for k in range(h * HU, (h + 1) * HU):
                        dve.wait_ge(s_gath[k], (i + rounds["L1C"] * G) * 16 + 16)
                    pl = ps[:, h, 0:32].rearrange("p (k f) -> p k f", f=4)
                    z = zE[:, h, :, :]
                    g = ring[:, h * HU:(h + 1) * HU, :]
                    s.link(V.tensor_tensor(z, g[:, :, 128:132], pl, ALU.add))
                    s.link(V.scalar_tensor_tensor(z, z, 0.2, z, ALU.mult, ALU.max))
                    s.link(V.tensor_tensor(z, z, g[:, :, 132:136], ALU.subtract))
                    dve.wait_ge(ph("L1C_exp"), i * 2 + h + 1)
                    s.link(V.tensor_tensor(z, pE[:, h, :, 0:4], g[:, :, 136:140], ALU.mult))
                    s.link(V.memset(g[:, :, 128:129], 1.0))
                    m = g[:, :, 0:F].rearrange("p k (h c) -> p k h c", h=4)
                    s.link(V.tensor_tensor(m, m, bc(z, 32), ALU.mult))
                    for k in range(h * HU, (h + 1) * HU):
                        b = node_block(1, i, k)
                        dve.wait_ge(ph("L1C_product"), i * U + U + k + 1)
                        dve.wait_ge(ph("L1C_added"), i * U + U + k)
                        part = acc[:, ds(b, 1), 0:129]
                        V.tensor_tensor(part, part, ps[:, 4 + k % 4, 0:129].unsqueeze(1), ALU.add).then_inc(ph("L1C_added"), 1)
            dve.wait_ge(sig("L1C", "_added"), all_added("L1C"))
            dve.wait_ge(ph("xl_table"), 32)
            link(V.tensor_copy(deg_in[:, :], acc[:, :, 128]))
            link(V.tensor_scalar(tmN[:, :], deg_in[:, :], 0.0, None, ALU.is_equal))
            link(V.tensor_tensor(xl, xl, bc(tmN[:, :], F), ALU.mult))
            link(V.tensor_tensor(x[:, :, :], x[:, :, :], acc[:, :, 0:F], ALU.add))
            link(V.tensor_tensor(x[:, :, :], x[:, :, :], xl, ALU.add))

            dve.sem_inc(ph("n2_transposed"), 1)
            dve.sem_inc(ph("n2_stored"), 1)
            N2 = NLN + 16
            with dve.Fori(0, CH) as i:
                s = Steps(dve, ph("n2_dve"), i, N2)
                dve.wait_ge(ph("n2_transposed"), i + 1)
                dve.wait_ge(ph("n2_stored"), i + 1)
                layer_norm(s, x[:, ds(i * CB, CB), :], lambda: dve.wait_ge(ph("n2_root"), i + 1))
                s.did(V.tensor_scalar(hs, hs, 0.0, None, ALU.max))
                dve.wait_ge(ph("n2_dve"), s.start + s.n)
                dve.sem_inc(ph("n2_filled"), 1)
                for h in range(4):
                    dve.wait_ge(ph("n2_qk"), i * 4 + h + 1)
                    for c, (b0, nb) in enumerate(((0, 3), (3, 2))):
                        pv = ps[:, 6 + c, 0:nb * 129].rearrange("p (b f) -> p b f", f=129)
                        s.did(V.tensor_copy(big[:, ds(i * CB + b0, nb), h * F:(h + 1) * F], pv[:, :, 0:F]))
                        s.did(V.tensor_copy(node1[:, ds(i * CB + b0, nb), h:h + 1], pv[:, :, F:F + 1]))
                s.end()
            link(V.memset(mx[:, :, :], -1e30))
            V.memset(acc[:, :, :].rearrange("p a b -> p (a b)"), 0.0).then_inc(ph("n2_free"), 1)
            dve.wait_ge(ph("n2_free"), 1)

            def sweep_scores(name):
                H = heads[name]
                same = H == 4
                with dve.Fori(0, G) as i:
                    for h in (0, 1):
                        halves(name, 1, i, h)
                        NS = 3 if same else 2
                        s = Steps(dve, ph(name + "_score"), i, NS * U, 2 * NS)
                        s.n = NS * h * HU
                        dve.wait_ge(sig(name, "_kept"), nth(name, i) * 2 + h + 1)
                        for k in range(h * HU, (h + 1) * HU):
                            one_hot(name, 1, i, k, True)
                            dve.wait_ge(sig(name, "_looked"), nth(name, i) * U + U + k + 1)
                            dve.wait_ge(s_gath[k], (i + rounds[name] * G) * 16 + 16)
                            q = ps[:, k % 2, 0:H * P].rearrange("p (h c) -> p h c", h=H)
                            g = ring[:, k, 0:F].unsqueeze(1).to_broadcast([P, H, F]) if same else \
                                ring[:, k, 0:H * F].rearrange("p (h c) -> p h c", h=H)
                            s.link(V.tensor_tensor(q, q, g, ALU.mult))
                            s.link(V.tensor_reduce(aS[:, k, 0:H], q, AX, ALU.add))
                            if same:
                                s.link(V.tensor_tensor(aS[:, k, 0:H], aS[:, k, 0:H], ps[:, 6 + k % 2, k * 4:k * 4 + 4], ALU.add))
                            if k % HU >= 2:
                                take_max(name, 1, i, k - 2)
                        for k in range((h + 1) * HU - 2, (h + 1) * HU):
                            take_max(name, 1, i, k)

            def sweep_values(name):
                H = heads[name]
                with dve.Fori(0, G) as i:
                    for h in (0, 1):
                        halves(name, 1, i, h)
                        for k in range(h * HU, (h + 1) * HU):
                            one_hot(name, 1, i, k)
                        dve.wait_ge(sig(name, "_looked"), nth(name, i) * U + U + (h + 1) * HU)
                        pl = ps[:, 6, h * 32:h * 32 + 32].rearrange("p (k f) -> p k f", f=4)
                        V.tensor_tensor(zE[:, h, :, 0:H], alpha[:, ds(i * U + h * HU, HU), 0:H], pl[:, :, 0:H],
                                        ALU.subtract).then_inc(sig(name, "_z"), 1)
                        for k in range(h * HU, (h + 1) * HU):
                            b = node_block(1, i, k)
                            dve.wait_ge(sig(name, "_product"), nth(name, i) * U + U + k + 1)
                            dve.wait_ge(sig(name, "_added"), nth(name, i) * U + U + k)
                            part = acc[:, ds(b, 1), 0:H * P]
                            V.tensor_tensor(part, part, ps[:, k % 4, 0:H * P].unsqueeze(1), ALU.add)
                            part = acc[:, ds(b, 1), 512:512 + H]
                            V.tensor_tensor(part, part, ps[:, 4 + k % 2, 0:H].unsqueeze(1), ALU.add).then_inc(sig(name, "_added"), 1)

            sweep_scores("L2A")
            dve.wait_ge(sig("L2A", "_added"), all_added("L2A"))
            sweep_values("L2C")
            dve.wait_ge(sig("L2C", "_added"), all_added("L2C"))

            dve.wait_ge(ph("wl2"), 128)
            link(V.tensor_scalar(wl2[:, :, 0:256], wl2[:, :, 0:256], ROOTD, None, ALU.mult))
            link(V.tensor_scalar(bl2[:, 0:256], bl2[:, 0:256], ROOTD, None, ALU.mult))
            dve.sem_inc(ph("wl2_scaled"), 1)
            dve.sem_inc(ph("n2b_stored"), 1)
            N2B = 4 + 3 * CB
            with dve.Fori(0, CH) as i:
                s = Steps(dve, ph("n2b_dve"), i, N2B)
                part = ds(i * CB, CB)
                r, f = stb[:, 0:CB, :], stb[:, CB:2 * CB, :]
                dve.wait_ge(ph("n2b_fl"), i + 1)
                s.link(V.tensor_scalar(f, acc[:, part, 512:516], 1e-16, None, ALU.add))
                s.link(V.reciprocal(r, f))
                s.link(V.tensor_tensor(f, acc[:, part, 512:516], r, ALU.mult))
                av = acc[:, part, 0:512].rearrange("p b (h c) -> p b h c", h=4)
                s.link(V.tensor_tensor(an, av, bc(r, F), ALU.mult))
                for b in range(CB):
                    dve.wait_ge(ph("n2b_mm"), (i * CB + b) + 1)
                    if b == 0:
                        dve.wait_ge(ph("n2b_stored"), i + 1)
                    s.did(V.tensor_tensor(q2[:, ds(i * CB + b, 1), :], ps[:, 6, 0:256].unsqueeze(1), bl2[:, 0:256].unsqueeze(1), ALU.add))
                    s.did(V.tensor_tensor(kv[:, b, 0:256], ps[:, 6, 256:512], bl2[:, 256:512], ALU.add))
                    s.did(V.tensor_tensor(kv[:, b, 256:512], ps[:, 7, 0:256], bl2[:, 512:768], ALU.add))
                    V.tensor_tensor(s2[:, ds(i * CB + b, 1), :], ps[:, 7, 256:384].unsqueeze(1), bl2[:, 768:896].unsqueeze(1),
                                    ALU.add).then_inc(ph("n2b_evac"), 1)
                dve.wait_ge(ph("n2b_evac"), i * CB + CB + 1)
                dve.sem_inc(ph("n2b_filled"), 1)
                s.end()
            link(V.memset(mx[:, :, :], -1e30))
            V.memset(acc[:, :, :].rearrange("p a b -> p (a b)"), 0.0).then_inc(ph("n2b_free"), 1)
            dve.wait_ge(ph("n2b_free"), 1)
            sweep_scores("L2D")
            dve.wait_ge(sig("L2D", "_added"), all_added("L2D"))
            sweep_values("L2F")
            dve.wait_ge(sig("L2F", "_added"), all_added("L2F"))
            lN = mx[:, :, 0:2]
            link(V.tensor_scalar(lN, acc[:, :, 512:514], 1e-16, None, ALU.add))
            link(V.reciprocal(lN, lN))
            link(V.tensor_scalar(lN, lN, 0.5, None, ALU.mult))
            for h in (0, 1):
                part = acc[:, :, h * F:(h + 1) * F]
                link(V.tensor_tensor(part, part, bc(mx[:, :, h], F), ALU.mult))
                link(V.tensor_tensor(x[:, :, :], x[:, :, :], part, ALU.add))
            link(V.tensor_tensor(x[:, :, :], x[:, :, :], s2, ALU.add))

            link(V.tensor_scalar(sums[:, :, 3], sums[:, :, 4], 1.0, None, ALU.max))
            V.tensor_scalar(deg_in[:, :], deg_in[:, :], 1.0, None, ALU.max).then_inc(ph("deg_ready"), 1)
            dve.wait_ge(ph("deg_root"), 1)
            link(V.reciprocal(sums[:, :, 2], sums[:, :, 1]))
            link(V.reciprocal(sums[:, :, 3], sums[:, :, 0]))
            link(V.memset(acc[:, :, :].rearrange("p a b -> p (a b)"), 0.0))
            dve.sem_inc(ph("n3_transposed"), 1)
            dve.sem_inc(ph("n3_stored"), 1)
            N3 = 2 * NLN + 4
            with dve.Fori(0, CH) as i:
                s = Steps(dve, ph("n3_dve"), i, N3)
                part = ds(i * CB, CB)
                dve.wait_ge(ph("n3_transposed"), i + 1)
                dve.wait_ge(ph("n3_stored"), i + 1)
                layer_norm(s, x[:, part, :], lambda: dve.wait_ge(ph("n3_root"), i * 2 + 1))
                s.link(V.tensor_scalar(hs, hs, 0.0, None, ALU.max))
                layer_norm(s, hs, lambda: dve.wait_ge(ph("n3_root"), i * 2 + 2))
                s.link(V.tensor_tensor(hs, hs, rows3[:, 0:1, :].to_broadcast([P, CB, F]), ALU.mult))
                s.link(V.tensor_tensor(hs, hs, rows3[:, 1:2, :].to_broadcast([P, CB, F]), ALU.add))
                s.link(V.tensor_tensor(vs, hs, bc(sums[:, part, 2], F), ALU.mult))
                dve.sem_inc(ph("n3_filled"), 1)
                s.link(V.tensor_tensor(x[:, part, :], x[:, part, :], rows3[:, 2:3, :].to_broadcast([P, CB, F]), ALU.add))
                dve.wait_ge(ph("n3_mm"), i + 2)
                s.link(V.tensor_tensor(x[:, part, :], x[:, part, :],
                                       psf[:, 1024:1024 + CN].rearrange("p (b f) -> p b f", f=F), ALU.add))
                s.end()
            dve.sem_inc(ph("n3_free"), 1)
            sweep_weighted("L3", 1, F, 0, False)
            dve.wait_ge(sig("L3", "_added"), all_added("L3"))
            dve.sem_inc(ph("n4_transposed"), 1)
            with dve.Fori(0, CH) as i:
                s = Steps(dve, ph("n4_dve"), i, 2)
                part = ds(i * CB, CB)
                dve.wait_ge(ph("n4_transposed"), i + 1)
                s.link(V.tensor_tensor(hs, acc[:, part, 0:F], bc(sums[:, part, 3], F), ALU.mult))
                dve.wait_ge(ph("n4_mm"), i + 2)
                s.link(V.tensor_tensor(x[:, part, :], x[:, part, :],
                                       psf[:, 1024:1024 + CN].rearrange("p (b f) -> p b f", f=F), ALU.add))
                s.end()
            dve.sem_inc(ph("final"), 1)

        @block.scalar
        def _(act):
            A = nc.scalar
            act.sem_inc(ph("n0_mm"), 1)
            act.sem_inc(ph("n0_stored"), 1)
            with act.Fori(0, CH) as i:
                act.wait_ge(ph("n0_dve"), i * NLN + VAR)
                A.activation(st[:, 32:32 + CB], st[:, 24:24 + CB], ACT.Sqrt).then_inc(ph("n0_root"), 1)
                act.wait_ge(ph("n0_transposed"), i + 2)
                act.wait_ge(ph("n0_mm"), i + 1)
                A.activation(hT, psf[:, 0:CN], ACT.Copy).then_inc(ph("n0_hT"), 1)
                act.wait_ge(ph("n0_mm"), i + 2)
                act.wait_ge(ph("n0_stored"), i + 1)
                A.activation(vs.rearrange("p b f -> p (b f)"), psf[:, 1024:1024 + CN], ACT.Copy).then_inc(ph("n0_evac"), 1)

            def rel_evac(o):
                act.wait_ge(s_relp, (o + 1))
                A.activation(relTs[0:TQ, :, :].rearrange("p q e -> p (q e)"), ps[0:TQ, 5, :], ACT.Copy).then_inc(s_rele, 1)

            rel_evac(0)
            act.wait_ge(s_relw, 16)
            rel_evac(1)
            act.wait_ge(s_w0, 128)
            with act.Fori(0, CH) as i:
                for hop in (0, 1):
                    act.wait_ge(ph("l0e_dve"), i * 30 + hop * 15 + 10)
                    A.activation(st[:, 32:32 + CB], st[:, 24:24 + CB], ACT.Sigmoid,
                                 bias=bf_b[:, hop:hop + 1]).then_inc(ph("l0e_gate"), 1)

            act.wait_ge(s_wt, NWT * 16)
            act.sem_inc(ph("n1_xlT"), 1)
            with act.Fori(0, CH) as i:
                act.wait_ge(ph("n1_dve"), i * (NLN + 3) + VAR)
                A.activation(st[:, 32:32 + CB], st[:, 24:24 + CB], ACT.Sqrt).then_inc(ph("n1_root"), 1)
                act.wait_ge(ph("n1_transposed"), i + 2)
                act.wait_ge(ph("n1_xlT"), i + 1)
                A.activation(hT, psf[:, 0:CN], ACT.Copy).then_inc(ph("n1_hT"), 1)
                act.wait_ge(ph("n1_xlT"), i + 2)
                A.activation(xlT, psf[:, 2048:2048 + CN], ACT.Identity, bias=blinT[:, 0:1]).then_inc(ph("n1_xlTe"), 1)

            def diagonals(name, i, k, src):
                act.wait_ge(sig(name, "_product"), nth(name, i) * U + U + k - 1)
                for hd in range(heads[name]):
                    ins = A.activation(wide[:, k % 2, hd * P:(hd + 1) * P], ident[:, :], ACT.Copy, scale=src[:, k, hd:hd + 1])
                ins.then_inc(sig(name, "_diag"), 1)

            with act.Fori(0, G) as i:
                for h in (0, 1):
                    for k in range(h * HU, (h + 1) * HU):
                        act.wait_ge(s_gath[k], (i + rounds["L1A"] * G) * 16 + 16)
                    A.activation(alpha[:, ds(i * U + h * HU, HU), :], ring[:, h * HU:(h + 1) * HU, 0:4], ACT.Copy)
                    for k in range(h * HU, (h + 1) * HU):
                        diagonals("L1A", i, k, ring)
            with act.Fori(0, G) as i:
                for h in (0, 1):
                    act.wait_ge(ph("L1B_dve"), i * 6 + h * 3 + 3)
                    act.wait_ge(ph("L1B_product"), i * U + (h + 1) * HU)
                    A.activation(pE[:, h, :, 0:4], zE[:, h, :, :], ACT.Exp).then_inc(ph("L1B_exp"), 1)
            with act.Fori(0, G) as i:
                for h in (0, 1):
                    act.wait_ge(ph("L1C_dve"), i * 12 + h * 6 + 3)
                    A.activation(pE[:, h, :, 0:4], zE[:, h, :, :], ACT.Exp).then_inc(ph("L1C_exp"), 1)

            act.wait_ge(s_wT, 1)
            act.wait_ge(s_wt, NWT * 16)
            A.activation(wkT[:, :, 0:F], ps[:, 0, :].rearrange("p (h f) -> p h f", h=4), ACT.Copy)
            A.activation(bq1T[:, :], bq1T[:, :], ACT.Copy, scale=ROOTD)
            A.activation(w3T[:, :, :].rearrange("p a b -> p (a b)"), ps[:, 1, 0:256], ACT.Copy).then_inc(s_wTe, 1)
            act.wait_ge(s_wTe, 1)
            act.sem_inc(ph("n2_q"), 1)
            with act.Fori(0, CH) as i:
                act.wait_ge(ph("n2_dve"), i * (NLN + 16) + VAR)
                A.activation(st[:, 32:32 + CB], st[:, 24:24 + CB], ACT.Sqrt).then_inc(ph("n2_root"), 1)
                act.wait_ge(ph("n2_transposed"), i + 2)
                act.wait_ge(ph("n2_q"), i * 4 + 1)
                A.activation(hT, psf[:, 0:CN], ACT.Copy).then_inc(ph("n2_hT"), 1)
                A.activation(h2T[:, ds(i * CN, CN)], psf[:, 0:CN], ACT.Copy).then_inc(ph("n2_hT"), 1)
                for h in range(4):
                    act.wait_ge(ph("n2_q"), i * 4 + h + 2)
                    A.activation(qT[:, h % 2, :], psf[:, 1024 * (1 + h % 2):1024 * (1 + h % 2) + CN], ACT.Identity,
                                 bias=bq1T[:, h:h + 1], scale=ROOTD).then_inc(ph("n2_qT"), 1)

            def sweep_scores(name):
                H = heads[name]
                NS = 3 if H == 4 else 2
                credit(act, name, "_kept", 2)
                with act.Fori(0, G) as i:
                    for h in (0, 1):
                        for k in range(h * HU, (h + 1) * HU):
                            act.wait_ge(ph(name + "_score"), (i * U + k + 3) * NS)
                            diagonals(name, i, k, aS)
                        A.activation(alpha[:, ds(i * U + h * HU, HU), 0:H], aS[:, h * HU:(h + 1) * HU, 0:H], ACT.Copy)\
                            .then_inc(sig(name, "_kept"), 1)

            def sweep_values(name):
                H = heads[name]
                with act.Fori(0, G) as i:
                    for h in (0, 1):
                        act.wait_ge(sig(name, "_z"), nth(name, i) * 2 + h + 1)
                        act.wait_ge(sig(name, "_product"), nth(name, i) * U + (h + 1) * HU)
                        A.activation(pE[:, h, :, 0:H], zE[:, h, :, 0:H], ACT.Exp).then_inc(sig(name, "_exp"), 1)
                        act.wait_ge(sig(name, "_exp"), nth(name, i) * 2 + h + 1)
                        for k in range(h * HU, (h + 1) * HU):
                            act.wait_ge(sig(name, "_product"), nth(name, i) * U + U + k - 1)
                            act.wait_ge(s_gath[k], (i + rounds[name] * G) * 16 + 16)
                            for hd in range(H):
                                row = ring[:, k, 0:F] if H == 4 else ring[:, k, hd * F:(hd + 1) * F]
                                ins = A.activation(wide[:, k % 2, hd * P:(hd + 1) * P], row, ACT.Copy,
                                                   scale=pE[:, h, k % HU, hd:hd + 1])
                            ins.then_inc(sig(name, "_value"), 1)

            sweep_scores("L2A")
            sweep_values("L2C")
            act.wait_ge(ph("wl2_scaled"), 1)
            with act.Fori(0, CH) as i:
                for h in range(4):
                    act.wait_ge(ph("n2b_aT"), i * 4 + h + 1)
                    A.activation(aT[:, h, :], psf[:, 0:CN], ACT.Copy).then_inc(ph("n2b_aTe"), 1)
                act.wait_ge(ph("n2b_fl"), i + 2)
                A.activation(flT[0:4, :], psf[0:4, 1024:1024 + CN], ACT.Copy).then_inc(ph("n2b_flT"), 1)
                for h in range(4):
                    act.wait_ge(ph("n2b_o"), i * 4 + h + 1)
                    A.activation(h1T[:, h, :], psf[:, 2048:2048 + CN], ACT.Relu, bias=bs1T[:, h:h + 1]).then_inc(ph("n2b_h1"), 1)
            sweep_scores("L2D")
            sweep_values("L2F")

            act.wait_ge(ph("deg_ready"), 1)
            A.activation(sums[:, :, 1], sums[:, :, 3], ACT.Sqrt)
            A.activation(sums[:, :, 0], deg_in[:, :], ACT.Sqrt).then_inc(ph("deg_root"), 1)
            act.sem_inc(ph("n3_mm"), 1)
            with act.Fori(0, CH) as i:
                for n in (0, 1):
                    act.wait_ge(ph("n3_dve"), i * (2 * NLN + 4) + n * NLN + VAR)
                    A.activation(st[:, 32:32 + CB], st[:, 24:24 + CB], ACT.Sqrt).then_inc(ph("n3_root"), 1)
                act.wait_ge(ph("n3_transposed"), i + 2)
                act.wait_ge(ph("n3_mm"), i + 1)
                A.activation(hT, psf[:, 0:CN], ACT.Copy).then_inc(ph("n3_hT"), 1)
            act.sem_inc(ph("n4_mm"), 1)
            with act.Fori(0, CH) as i:
                act.wait_ge(ph("n4_transposed"), i + 2)
                act.wait_ge(ph("n4_mm"), i + 1)
                A.activation(hT, psf[:, 0:CN], ACT.Copy).then_inc(ph("n4_hT"), 1)


        @block.tensor
        def _(pe):
            M = nc.tensor

            def prefix(o):
                pe.wait_ge(v_s[o], (PRE if o == 0 else 0) + 8 + KB * 5)
                M.matmul(ps[:, 6, 0:KB], lower, cnt, start=True, stop=True)
                M.matmul(ps[:, 7, 0:KB], ones, cnt, start=True, stop=True).then_inc(s_pref, 1)

            def rel_transpose(o):
                pe.wait_ge(s_relf, (o + 1) * 2)
                for q in range(4):
                    last = M.transpose(ps[0:TQ, 5, q * P:(q + 1) * P], relF[:, q * TQ:(q + 1) * TQ], ident[:, :])
                last.then_inc(s_relp, 1)

            def sweep(name, width):
                credit(pe, name, "_product", U)
                with pe.Fori(0, G) as i:
                    for k in range(U):
                        pe.wait_ge(sig(name, "_onehot"), nth(name, i) * U + k + 1)
                        pe.wait_ge(s_gath[k], (i + rounds[name] * G) * 16 + 16)
                        pe.wait_ge(sig(name, "_added"), nth(name, i) * U + U - 8 + k + 1)
                        M.matmul(ps[:, k % 8, 0:width], oh[:, k, :], ring[:, k, 0:width],
                                 start=True, stop=True).then_inc(sig(name, "_product"), 1)

            pe.wait_ge(s_cst, 9)
            prefix(0)
            pe.wait_ge(s_w0, 128)
            pe.sem_inc(ph("n0_evac"), 1)
            with pe.Fori(0, CH) as i:
                pe.wait_ge(ph("n0_dve"), i * NLN + NLN)
                for b in range(CB):
                    last = M.transpose(psf[:, b * P:(b + 1) * P], hs[:, b, :], ident[:, :])
                last.then_inc(ph("n0_transposed"), 1)
                pe.wait_ge(ph("n0_hT"), i + 1)
                pe.wait_ge(ph("n0_evac"), i + 1)
                for b in range(CB):
                    last = M.matmul(psf[:, 1024 + b * P:1024 + (b + 1) * P], hT[:, b * P:(b + 1) * P], w01[:, :],
                                    start=True, stop=True)
                last.then_inc(ph("n0_mm"), 1)
            prefix(1)
            rel_transpose(0)
            pe.wait_ge(s_rele, 1)
            pe.wait_ge(ph("L0_ones"), 1)
            sweep("L0h1", 129)
            rel_transpose(1)
            pe.wait_ge(s_rele, 2)
            sweep("L0h2", 65)


            def transposes():
                for b in range(CB):
                    last = M.transpose(psf[:, b * P:(b + 1) * P], hs[:, b, :], ident[:, :])
                return last

            def by_block(weights):
                for b in range(CB):
                    last = M.matmul(psf[:, 1024 + b * P:1024 + (b + 1) * P], hT[:, b * P:(b + 1) * P], weights,
                                    start=True, stop=True)
                return last

            def by_nodes(at, pairs):
                for c, w in ((0, 512), (512, CN - 512)):
                    for n, (wt, mv) in enumerate(pairs):
                        last = M.matmul(psf[:, at + c:at + c + w], wt, mv(c, w), start=n == 0, stop=n == len(pairs) - 1)
                return last

            def block_of(o, i, k):
                return pe.value_load(blk[o][0:1, ds(i * U + k, 1)], min_val=0, max_val=NB - 1)

            pe.wait_ge(s_wt, NWT * 16)
            with pe.Fori(0, CH) as i:
                pe.wait_ge(ph("n1_dve"), i * (NLN + 3) + NLN)
                transposes().then_inc(ph("n1_transposed"), 1)
                pe.wait_ge(ph("n1_hT"), i + 1)
                by_block(wlin[:, :]).then_inc(ph("n1_mm"), 1)
                by_nodes(2048, [(wlin[:, :], lambda c, w: hT[:, c:c + w])]).then_inc(ph("n1_xlT"), 1)
                pe.wait_ge(ph("n1_xlTe"), i + 1)
                for b in range(CB):
                    last = M.matmul(psf[:, 3072 + b * 8:3072 + b * 8 + 8], xlT[:, b * P:(b + 1) * P], watt[:, :], start=True, stop=True)
                last.then_inc(ph("n1_att"), 1)

            def tile_max(name, i, k):
                H = heads[name]
                pe.wait_ge(sig(name, "_onehot"), nth(name, i) * U + k + 1)
                pe.wait_ge(sig(name, "_diag"), nth(name, i) * U + k + 1)
                pe.wait_ge(sig(name, "_added"), nth(name, i) * U + U - 4 + k + 1)
                M.matmul(ps[:, 2 + k % 4, 0:H * P], oh[:, k, :], wide[:, k % 2, 0:H * P], start=True, stop=False)
                M.matmul(ps[:, 2 + k % 4, 0:H * P].rearrange("p (h e) -> p h e", h=H), ohm[:, k, :],
                         ident_b[:, :].unsqueeze(1).to_broadcast([P, H, P]), start=False, stop=True)\
                    .then_inc(sig(name, "_product"), 1)

            pe.wait_ge(ph("n1_done"), 1)
            pe.sem_inc(ph("L1A_product"), U)
            with pe.Fori(0, G) as i:
                for k in range(U):
                    tile_max("L1A", i, k)

            pe.sem_inc(ph("L1B_product"), U)
            pe.sem_inc(ph("L1B_looked"), U)
            pe.sem_inc(ph("L1B_added"), U)
            with pe.Fori(0, G) as i:
                for h in (0, 1):
                    pe.wait_ge(ph("L1B_ohT"), i * 2 + h + 3)
                    for k in range(HU):
                        b = block_of(0, i, h * HU + k)
                        M.matmul(ps[:, h, k * 8:k * 8 + 8].unsqueeze(1), ohT[:, h, k * P:(k + 1) * P], node1[:, ds(b, 1), 0:8],
                                 start=True, stop=True).then_inc(ph("L1B_looked"), 1)
                    pe.wait_ge(ph("L1B_onehot"), i * U + (h + 1) * HU)
                    pe.wait_ge(ph("L1B_exp"), i * 2 + h + 1)
                    pe.wait_ge(ph("L1B_added"), i * U + (h + 1) * HU)
                    for k in range(HU):
                        M.matmul(ps[:, 2 + h, k * 8:k * 8 + 5], oh[:, h * HU + k, :], pE[:, h, k, :],
                                 start=True, stop=True).then_inc(ph("L1B_product"), 1)

            pe.sem_inc(ph("L1C_product"), U)
            pe.sem_inc(ph("L1C_looked"), U)
            with pe.Fori(0, G) as i:
                for h in (0, 1):
                    pe.wait_ge(ph("L1C_ohT"), i * 2 + h + 3)
                    for k in range(HU):
                        b = block_of(1, i, h * HU + k)
                        M.matmul(ps[:, h, k * 4:k * 4 + 4].unsqueeze(1), ohT[:, h, k * P:(k + 1) * P], node1[:, ds(b, 1), 12:16],
                                 start=True, stop=True).then_inc(ph("L1C_looked"), 1)
                    pe.wait_ge(ph("L1C_onehot"), i * U + (h + 1) * HU)
                    pe.wait_ge(ph("L1C_dve"), i * 12 + h * 6 + 6)
                    for k in range(h * HU, (h + 1) * HU):
                        pe.wait_ge(ph("L1C_added"), i * U + U - 4 + k + 1)
                        M.matmul(ps[:, 4 + k % 4, 0:129], oh[:, k, :], ring[:, k, 0:129],
                                 start=True, stop=True).then_inc(ph("L1C_product"), 1)

            pe.wait_ge(sig("L1C", "_added"), all_added("L1C"))
            pe.wait_ge(ph("wraw"), 32)
            for h in range(4):
                M.transpose(ps[:, 0, h * P:(h + 1) * P], wk1[:, h * P:(h + 1) * P], ident[:, :])
            for h in range(2):
                last = M.transpose(ps[:, 1, h * P:(h + 1) * P], w3[:, h * P:(h + 1) * P], ident[:, :])
            last.then_inc(s_wT, 1)
            pe.wait_ge(s_wTe, 1)
            with pe.Fori(0, CH) as i:
                pe.wait_ge(ph("n2_dve"), i * (NLN + 16) + NLN)
                transposes().then_inc(ph("n2_transposed"), 1)
                pe.wait_ge(ph("n2_hT"), i * 2 + 2)
                for h in range(4):
                    at = 1024 * (1 + h % 2)
                    by_nodes(at, [(wq1[:, h * P:(h + 1) * P], lambda c, w: hT[:, c:c + w])]).then_inc(ph("n2_q"), 1)
                    pe.wait_ge(ph("n2_qT"), i * 4 + h + 1)
                    if h:
                        pe.wait_ge(ph("n2_dve"), i * (NLN + 16) + NLN + 4 * h)
                    for b in range(CB):
                        c = (b % 3) * 129
                        last = M.matmul(ps[:, 6 + b // 3, c:c + 129], qT[:, h % 2, b * P:(b + 1) * P], wkT[:, h, :], start=True, stop=True)
                    last.then_inc(ph("n2_qk"), 1)

            def sweep_scores(name, table):
                H = heads[name]
                credit(pe, name, "_product", U)
                credit(pe, name, "_looked", U)
                NS = 3 if H == 4 else 2
                pe.sem_inc(ph(name + "_score"), 2 * NS)

                with pe.Fori(0, G) as i:
                    for h in (0, 1):
                        pe.wait_ge(sig(name, "_ohT"), nth(name, i) * 2 + h + 3)
                        for k in range(h * HU, (h + 1) * HU):
                            pe.wait_ge(ph(name + "_score"), (i * U + k + 1) * NS)
                            b = block_of(1, i, k)
                            w = ohT[:, h, (k % HU) * P:(k % HU + 1) * P]
                            ins = M.matmul(ps[:, k % 2, 0:H * P].unsqueeze(1), w, table(b), start=True, stop=True)
                            if H == 4:
                                ins = M.matmul(ps[:, 6 + k % 2, k * 4:k * 4 + 4].unsqueeze(1), w, node1[:, ds(b, 1), 0:4], start=True, stop=True)
                            ins.then_inc(sig(name, "_looked"), 1)
                            if k % HU:
                                tile_max(name, i, k - 1)
                        tile_max(name, i, (h + 1) * HU - 1)

            def sweep_values(name):
                H = heads[name]
                credit(pe, name, "_product", U)
                credit(pe, name, "_looked", U)
                with pe.Fori(0, G) as i:
                    for h in (0, 1):
                        pe.wait_ge(sig(name, "_ohT"), nth(name, i) * 2 + h + 3)
                        for k in range(h * HU, (h + 1) * HU):
                            b = block_of(1, i, k)
                            w = ohT[:, h, (k % HU) * P:(k % HU + 1) * P]
                            M.matmul(ps[:, 6, k * 4:k * 4 + H].unsqueeze(1), w, mx[:, ds(b, 1), 0:H], start=True, stop=True)\
                                .then_inc(sig(name, "_looked"), 1)
                        pe.wait_ge(sig(name, "_onehot"), nth(name, i) * U + (h + 1) * HU)
                        for k in range(h * HU, (h + 1) * HU):
                            pe.wait_ge(sig(name, "_value"), nth(name, i) * U + k + 1)
                            pe.wait_ge(sig(name, "_added"), nth(name, i) * U + U - 2 + k + 1)
                            M.matmul(ps[:, k % 4, 0:H * P], oh[:, k, :], wide[:, k % 2, 0:H * P], start=True, stop=True)
                            M.matmul(ps[:, 4 + k % 2, 0:H], oh[:, k, :], pE[:, h, k % HU, 0:H], start=True, stop=True)\
                                .then_inc(sig(name, "_product"), 1)

            pe.wait_ge(ph("n2_free"), 1)
            sweep_scores("L2A", lambda b: big[:, ds(b, 1), :])
            sweep_values("L2C")
            pe.wait_ge(ph("wl2_scaled"), 1)
            pe.sem_inc(ph("n2b_fl"), 1)
            pe.sem_inc(ph("n2b_evac"), 1)
            with pe.Fori(0, CH) as i:
                first = i * (4 + 3 * CB)
                pe.wait_ge(ph("n2b_dve"), first + 4)
                for h in range(4):
                    if h:
                        pe.wait_ge(ph("n2b_aTe"), i * 4 + h)
                    for b in range(CB):
                        last = M.transpose(psf[:, b * P:(b + 1) * P], an[:, b, h, :], ident[:, :])
                    last.then_inc(ph("n2b_aT"), 1)
                for b in range(CB):
                    last = M.transpose(psf[0:4, 1024 + b * P:1024 + (b + 1) * P], stb[:, CB + b, :], ident[:, :])
                last.then_inc(ph("n2b_fl"), 1)
                pe.wait_ge(ph("n2b_aTe"), i * 4 + 4)
                pe.wait_ge(ph("n2b_flT"), i + 1)
                for h in range(4):
                    if h:
                        pe.wait_ge(ph("n2b_h1"), i * 4 + h)
                    by_nodes(2048, [(wv1[:, h * P:(h + 1) * P], lambda c, w: aT[:, h, c:c + w]),
                                    (ws1[:, h * P:(h + 1) * P], lambda c, w: h2T[:, ds(i * CN + c, w)]),
                                    (bv4[:, h, :], lambda c, w: flT[0:4, c:c + w])]).then_inc(ph("n2b_o"), 1)
                pe.wait_ge(ph("n2b_h1"), i * 4 + 4)
                for b in range(CB):
                    pe.wait_ge(ph("n2b_evac"), i * CB + b + 1)
                    for h in range(4):
                        M.matmul(ps[:, 6, :], h1T[:, h, b * P:(b + 1) * P], wl2[:, h, 0:512], start=h == 0, stop=h == 3)
                    for h in range(4):
                        last = M.matmul(ps[:, 7, 0:384], h1T[:, h, b * P:(b + 1) * P], wl2[:, h, 512:896], start=h == 0, stop=h == 3)
                    last.then_inc(ph("n2b_mm"), 1)
            pe.wait_ge(ph("n2b_free"), 1)
            sweep_scores("L2D", lambda b: q2[:, ds(b, 1), :])
            sweep_values("L2F")

            with pe.Fori(0, CH) as i:
                pe.wait_ge(ph("n3_dve"), i * (2 * NLN + 4) + 2 * NLN + 1)
                transposes().then_inc(ph("n3_transposed"), 1)
                pe.wait_ge(ph("n3_hT"), i + 1)
                by_block(w3T[:, 0, :]).then_inc(ph("n3_mm"), 1)
            sweep("L3", F)
            with pe.Fori(0, CH) as i:
                pe.wait_ge(ph("n4_dve"), i * 2 + 1)
                transposes().then_inc(ph("n4_transposed"), 1)
                pe.wait_ge(ph("n4_hT"), i + 1)
                by_block(w3T[:, 1, :]).then_inc(ph("n4_mm"), 1)


_INS = ['x', 'src', 'dst', 'edge_weight', 'L0_gnn_W0', 'L0_gnn_b0', 'L0_gnn_W1', 'L0_gnn_b1', 'L0_gnn_fc0', 'L0_gnn_bf0', 'L0_gnn_fc1', 'L0_gnn_bf1', 'L1_gnn_W_lin', 'L1_gnn_b_lin', 'L1_gnn_W_att', 'L1_gnn_b_att', 'L2_gnn_Wq1', 'L2_gnn_bq1', 'L2_gnn_Wk1', 'L2_gnn_bk1', 'L2_gnn_Wv1', 'L2_gnn_bv1', 'L2_gnn_Ws1', 'L2_gnn_bs1', 'L2_gnn_Wq2', 'L2_gnn_bq2', 'L2_gnn_Wk2', 'L2_gnn_bk2', 'L2_gnn_Wv2', 'L2_gnn_bv2', 'L2_gnn_Ws2', 'L2_gnn_bs2', 'L3_gnn_ln_gamma', 'L3_gnn_ln_beta', 'L3_gnn_W', 'L3_gnn_b']


def kernel(**inputs):
    import numpy as _np
    import concourse.bacc as _bacc
    from concourse import mybir as _mybir
    from concourse.bass_utils import run_bass_kernel_spmd as _run

    nc = _bacc.Bacc("TRN2", target_bir_lowering=False, num_devices=1)
    arrays, args = {}, {}
    for name in _INS:
        v = _np.ascontiguousarray(inputs[name])
        arrays[f"in_{name}_dram"] = v
        args[name] = nc.dram_tensor(f"in_{name}_dram", v.shape, _mybir.dt.from_np(v.dtype), kind="ExternalInput").ap()
    out = nc.dram_tensor("out_0_dram", inputs["x"].shape, _mybir.dt.float32, kind="ExternalOutput").ap()
    gnn_stack(nc, args, out)
    r = _run(nc, [arrays], core_ids=[0])
    return r.results[0]["out_0_dram"]
```

```python
import concourse.bass as bass
from concourse import mybir
from contextlib import ExitStack


class Steps:

    def __init__(self, eng, sem, i, per, first=0):
        self.eng, self.sem, self.start, self.per, self.n = eng, sem, i * per + first, per, 0

    def did(self, ins):
        self.n += 1
        ins.then_inc(self.sem, 1)

    def link(self, ins):
        self.did(ins)
        self.eng.wait_ge(self.sem, self.start + self.n)

    def end(self):
        assert self.n == self.per, (self.n, self.per)


def gnn_stack(nc, a, out):
    f32, bf16, i32 = mybir.dt.float32, mybir.dt.bfloat16, mybir.dt.int32
    ALU, ACT, AX = mybir.AluOpType, mybir.ActivationFunctionType, mybir.AxisListType.X
    ds = bass.ds
    x_in, src_in, dst_in, w_in = a["x"], a["src"], a["dst"], a["edge_weight"]

    P, F = 128, 128
    N, E = x_in.shape[0], src_in.shape[0]
    NB = -(-N // P)
    NFULL = N // P
    NREST = N - NFULL * P
    NP = NB * P
    J = 400
    EP = E // J
    U = 16
    HU = U // 2
    QU = U // 4
    G = -(-(E // P + NB) // U)
    T = G * U
    TP = T + 1 + (P * J - E) // P
    KB = NB + 1
    CB = 5
    CH = NB // CB
    CN = CB * P
    BIG = float(2.0 ** 120)
    assert EP * J == E and CH * CB == NB and J % U == 0 and T >= (E + NB * (P - 1)) // P

    ctx = ExitStack()
    with ctx:
        def sb(name, shape, dt=f32):
            return ctx.enter_context(nc.sbuf_tensor(name, shape, dt))

        def sem(name):
            return ctx.enter_context(nc.semaphore(name))

        def dram(name, shape, dt=f32):
            return nc.dram_tensor(name, shape, dt, kind="Internal").ap()

        RW = (3, 2)
        rec_dram = [dram("rec_by_src", [P * TP, RW[0]]), dram("rec_by_dst", [P * TP, RW[1]])]
        relT_dram = [dram("relT_by_src", [T, P], bf16), dram("relT_by_dst", [T, P], bf16)]
        t_v0 = dram("t_v0", [NP, F])
        t_v1 = dram("t_v1", [NP, 65])
        t_sj = dram("t_sj", [NP, 4])
        t_xl = dram("t_xl", [NP, 140])
        t_h2 = dram("t_h2", [NP, F])
        t_k2 = dram("t_k2", [NP, 256])
        t_v2 = dram("t_v2", [NP, 256])
        t_h3 = dram("t_h3", [NP, F])

        x = sb("x_nodes", [P, NB, F])
        acc = sb("acc", [P, NB, 516])
        big = sb("big", [P, NB, 512])
        h2T = sb("h2T", [P, NP])
        rec = [sb("rec_s", [P, T, RW[0]]), sb("rec_d", [P, T, RW[1]])]
        last_tile = [sb("last_tile_s", [P, KB], i32), sb("last_tile_d", [P, KB], i32)]
        blk = [sb("block_of_tile_s", [P, T], i32), sb("block_of_tile_d", [P, T], i32)]
        alpha = sb("alpha", [P, T, 4])
        ident = sb("ident", [P, P])
        iota_f = sb("iota_f", [P, P])
        pidx = sb("pidx", [P, 1])
        WORK = 11264
        work = sb("work", [P, WORK])

        def carve(at, shape, dt=f32):
            n = 1
            for s in shape:
                n *= s
            words = n if dt in (f32, i32) else n // 2
            v = work[:, at:at + words]
            if dt != f32:
                v = v.bitcast(dt)
            if len(shape) == 2:
                v = v.rearrange("p (a b) -> p a b", a=shape[0])
            if len(shape) == 3:
                v = v.rearrange("p (a b c) -> p a b c", a=shape[0], b=shape[1])
            return v

        ring = carve(0, [U, 256])
        oh = carve(4096, [U, P])
        ohm = carve(6144, [U, P], bf16)
        wide = carve(7168, [2, 512])
        ohT = carve(8192, [2, HU * P])
        relB = carve(10240, [2, HU * P], bf16)
        ohTb = carve(8192, [2, HU * P], bf16)
        pA = carve(10144, [2, HU, 4])
        p3 = carve(9216, [2 * HU, 13], bf16)
        looked = carve(9344, [2, HU * 8])
        ohTq = carve(4096, [2, HU * P], bf16)
        spread = carve(5120, [2, 512], bf16)
        score3 = carve(5632, [2, 96], bf16)
        pick = carve(7168, [HU, P], bf16)
        low_id = carve(7680, [P], bf16)
        of_head = carve(7744, [4])
        lookedQ = carve(7760, [2, HU * 4])
        rowno = carve(7824, [2])
        accf = acc[:, :, :].rearrange("p a b -> p (a b)")
        node24 = accf[:, 0:300].bitcast(bf16).rearrange("p (b c f) -> p b c f", b=NB, c=3)
        node12 = accf[:, 512:662].bitcast(bf16).rearrange("p (b c f) -> p b c f", b=NB, c=3)
        tile_mx = accf[:, 2048:2048 + T * 4].rearrange("p (t h) -> p t h", h=4)
        run_mx = accf[:, 4096:4096 + T * 4].rearrange("p (t h) -> p t h", h=4)
        starts = accf[:, 6144:6144 + T]
        mx12 = carve(9984, [NB, 3 * 4], bf16)
        mrest = carve(7168, [NB, 4])
        rest = accf[:, 1024:1024 + NB * 8].rearrange("p (b f) -> p b f", b=NB)
        hs = carve(0, [CB, F])
        xc = carve(640, [CB, F])
        sq = carve(1280, [CB, F])
        hT = carve(1920, [CN])
        vs = carve(2560, [CB, F])
        st = sb("st", [P, 64])
        idx_slot = sb("idx_slot", [P, U], i32)

        ps = ctx.enter_context(nc.psum_tensor("ps", [P, 8, 512], f32))
        psf = ps[:, :, :].rearrange("p a b -> p (a b)")
        psum_blocks = psf[:, 0:NP].rearrange("p (b f) -> p b f", f=P)

        bigf = big[:, :, :].rearrange("p a b -> p (a b)")
        kI, oI = bigf[:, 0:J].bitcast(i32), bigf[:, J:2 * J].bitcast(i32)
        wF = bigf[:, 2 * J:3 * J]
        tI = bigf[:, 3 * J:4 * J].bitcast(i32)
        blkF = bigf[:, 4 * J:5 * J]
        msk, cum, tmp = (bigf[:, n * J:(n + 1) * J] for n in (5, 6, 7))
        zeros = bigf[:, 8 * J:9 * J]
        rank = [bigf[:, 9 * J:10 * J], bigf[:, 10 * J:11 * J]]
        rowI = [bigf[:, n * J:(n + 1) * J].bitcast(i32) for n in (11, 12)]
        recE = [bigf[:, (13 + 4 * o) * J:(13 + 4 * o + RW[o]) * J].rearrange("p (j w) -> p j w", w=RW[o]) for o in (0, 1)]
        tf = bigf[:, 21 * J:22 * J]
        o0 = 22 * J
        relF = bigf[:, o0:o0 + T]
        mapF = bigf[:, o0 + T:o0 + 2 * T]
        iotaT = bigf[:, o0 + 2 * T:o0 + 3 * T]
        relTs = bigf[:, o0 + 3 * T:o0 + 3 * T + 256].bitcast(bf16).rearrange("p (q e) -> p q e", q=4)
        o1 = o0 + 3 * T + 256
        bval = bigf[:, o1:o1 + KB]
        cnt = bigf[:, o1 + 32:o1 + 32 + KB]
        til = bigf[:, o1 + 64:o1 + 64 + KB]
        tilI = bigf[:, o1 + 96:o1 + 96 + KB].bitcast(i32)
        end_ = bigf[:, o1 + 128:o1 + 128 + KB]
        base = bigf[:, o1 + 160:o1 + 160 + KB]
        lower = bigf[:, o1 + 192:o1 + 192 + P]
        ones = bigf[:, o1 + 320:o1 + 320 + P]
        fill = [acc[:, 4 * o:4 * o + 4, :].rearrange("p a b -> p (a b)")[:, 0:TP * RW[o]] for o in (0, 1)]
        assert o1 + 448 + 2 * T <= NB * 512
        sc_idx = sb("sc_idx", [P, U], i32)
        sc_rec = [sb("sc_rec_s", [P, U, RW[0]]), sb("sc_rec_d", [P, U, RW[1]])]
        mapI = [bigf[:, o1 + 448 + o * T:o1 + 448 + (o + 1) * T].bitcast(i32) for o in (0, 1)]
        TQ = T // 4

        node1 = sb("node1", [P, NB, 16])
        mx = sb("mx", [P, NB, 4])
        sums = sb("sums", [P, NB, 5])
        tmN = sb("tmN", [P, NB])
        stb = sb("stb", [P, 2 * CB, 4])
        deg_in = sb("deg_in", [P, NB])
        zero_b = carve(9728, [512], bf16)
        w3b = carve(10240, [T, 3], bf16)
        wrest = carve(9216, [T])
        pE = sb("pE", [P, 2, HU, 5])
        zE = sb("zE", [P, 2, HU, 4])
        aS = sb("aS", [P, U, 4])
        tm = sb("tm", [P, 4, 4])
        ident_b = sb("ident_b", [P, P], bf16)
        xl = bigf[:, 0:NP].rearrange("p (b f) -> p b f", f=F)
        q2 = bigf[:, 0:2 * NP].rearrange("p (b f) -> p b f", f=256)
        s2 = bigf[:, 2 * NP:3 * NP].rearrange("p (b f) -> p b f", f=F)
        kv = bigf[:, 3 * NP:3 * NP + CB * 512].rearrange("p (b f) -> p b f", f=512)
        xlT = carve(3200, [CN])
        qT = carve(3840, [2, CN])
        aT = carve(0, [4, CN])
        h1T = carve(2560, [4, CN])
        flT = carve(5120, [CN])
        wl2 = carve(5760, [4, 896])
        bl2 = carve(9344, [896])
        an = h1T.rearrange("p a b -> p (a b)").rearrange("p (b h c) -> p b h c", b=CB, h=4)

        wlin = h2T[:, 384:512]
        watt = sb("watt", [P, 8])
        blinT = sb("blinT", [P, 1])
        battb = sb("battb", [P, 4])
        wq1 = sb("wq1", [P, 512])
        wk1 = carve(5120, [512])
        wv1 = sb("wv1", [P, 512])
        ws1 = sb("ws1", [P, 512])
        wkT = sb("wkT", [P, 4, 129])
        bq1T = sb("bq1T", [P, 4])
        bs1T = sb("bs1T", [P, 4])
        bv4 = sb("bv4", [4, 4, 128])
        w3 = carve(5632, [256])
        w3T = sb("w3T", [P, 2, 128])
        rows3 = sb("rows3", [P, 4, 128])
        w01 = h2T[:, 0:128]
        brow = h2T[:, 128:384].rearrange("p (a b) -> p a b", a=2)
        bf_b = sb("bf_b", [P, 2])

        s_cst = sem("constants_ready")
        s_x = sem("x_loaded")
        s_xz = sem("x_zeroed")
        s_key = sem("edges_loaded")
        s_w0 = sem("weights0_loaded")
        s_pad = sem("pads_set")
        s_filled = sem("rec_dram_filled")
        v_s = [sem("sort_dve_s"), sem("sort_dve_d")]
        s_pref = sem("prefix")
        s_pos = sem("rows_ready")
        s_cp = sem("scatter_slots_filled")
        s_sc = [sem("scatter_half0"), sem("scatter_half1")]
        s_scd = sem("scatter_order_done")
        s_gate = sem("pool_gate")
        s_rec = sem("rec_back")
        s_relf = sem("rel_compact")
        s_relp = sem("rel_transposed")
        s_rele = sem("rel_evac")
        s_relw = sem("rel_written")
        s_gath = [sem(f"gathered{k}") for k in range(4)]
        s_out = sem("out_written")
        s_wt = sem("weights_loaded")
        s_wT = sem("weights_transposed")
        s_wTe = sem("weights_transposed_copied")
        NWT = 28

        block = ctx.enter_context(nc.Block())

        NLN = 9
        VAR = 6
        PRE = 7

        def table_rows(t, i):
            return t[ds(i * CN, CN), :].rearrange("(b p) f -> p b f", p=P)

        made = {}

        def ph(name):
            if name not in made:
                made[name] = sem(name)
            return made[name]

        EARLIER = {"L0h2": ("L0h1", 1), "L3": ("L0h1", 2), "L1C": ("L1B", 1), "L2A": ("L1A", 1), "L2D": ("L1A", 2),
                   "L2Dq": ("L2Aq", 1), "L2F": ("L2C", 1)}

        def sig(name, what):
            return ph(EARLIER.get(name, (name, 0))[0] + what)

        def nth(name, i):
            return i + EARLIER.get(name, (name, 0))[1] * G

        def credit(eng, name, what, n):
            if name not in EARLIER:
                eng.sem_inc(sig(name, what), n)

        rounds = {n: r for r, n in enumerate(("L0h1", "L0h2", "L1A", "L1C", "L2A", "L2C", "L2D", "L2F", "L3"))}
        rel_rounds = {n: r for r, n in enumerate(("L1B", "L1C", "L2A", "L2C", "L2D", "L2F"))}
        heads = {"L1A": 4, "L2A": 4, "L2C": 4, "L2D": 2, "L2F": 2}
        for n in ("L2A", "L2D"):
            rel_rounds[n + "q"] = rel_rounds[n]
        s_relB = [sem("rel_rows0"), sem("rel_rows1")]
        ROOTD = float(F) ** -0.5
        MAXES = ("L1A", "L2A", "L2D")
        SUMS = ("L0h1", "L0h2", "L1C", "L3")


        def loaded_blocks(engine, o, i, h):
            return [b for c in (0, QU) for b in nc.values_load_multi_w_load_instructions(
                blk[o][0:1, ds(i * U + h * HU + c, QU)], engines=[engine], min_val=0, max_val=NB - 1,
                skip_runtime_bounds_check_because="the sort counts block ends and takes the minimum with NB - 1")[1]]

        def before(i, h):
            return (i, 0) if h else (i - 1, 1)

        def passes(eng, half):
            half(0, 0, True, False)
            half(0, 1, False, False)
            with eng.Fori(1, G - 1) as i:
                half(i, 0, False, False)
                half(i, 1, False, False)
            half(G - 1, 0, False, False)
            half(G - 1, 1, False, True)

        def with_next(eng, half):
            with eng.Fori(0, G - 1) as i:
                half(i, 0, (i, 1))
                half(i, 1, (i + 1, 0))
            half(G - 1, 0, (G - 1, 1))
            half(G - 1, 1, None)

        def ahead(eng, first, then):
            first(0, 0)
            with eng.Fori(0, G - 1) as i:
                first(i, 1)
                then(i, 0)
                first(i + 1, 0)
                then(i, 1)
            first(G - 1, 1)
            then(G - 1, 0)
            then(G - 1, 1)

        @block.sync
        def _(sp):
            sp.wait_ge(s_pad, 1)
            sp.dma_start(kI[0:EP, :], src_in.rearrange("(p j) -> p j", j=J)).then_inc(s_key, 16)
            sp.dma_start(oI[0:EP, :], dst_in.rearrange("(p j) -> p j", j=J)).then_inc(s_key, 16)
            sp.dma_start(wF[0:EP, :], w_in.rearrange("(p j) -> p j", j=J)).then_inc(s_key, 16)
            sp.wait_ge(s_xz, 1)
            sp.dma_start(x[:, 0:NFULL, :], x_in[0:NFULL * P, :].rearrange("(b p) f -> p b f", p=P)).then_inc(s_x, 16)
            sp.dma_start(x[0:NREST, NFULL, :], x_in[NFULL * P:N, :]).then_inc(s_x, 16)
            sp.dma_start(w01[:, 0:64], a["L0_gnn_W0"]).then_inc(s_w0, 16)
            sp.dma_start(w01[:, 64:128], a["L0_gnn_W1"]).then_inc(s_w0, 16)
            for n, nm in enumerate(("b0", "b1", "fc0", "fc1")):
                v = a["L0_gnn_" + nm]
                v = v if n < 2 else v.rearrange("a b -> (a b)")
                sp.dma_start(brow[:, n // 2, (n % 2) * 64:(n % 2) * 64 + 64], v.partition_broadcast(P)).then_inc(s_w0, 16)
            for n in (0, 1):
                sp.dma_start(bf_b[:, n:n + 1], a[f"L0_gnn_bf{n}"].partition_broadcast(P)).then_inc(s_w0, 16)
            wts = [(wlin[:, :], a["L1_gnn_W_lin"]),
                   (watt[:, 0:4], a["L1_gnn_W_att"][0:F, :]), (watt[:, 4:8], a["L1_gnn_W_att"][F:2 * F, :]),
                   (blinT[:, :], a["L1_gnn_b_lin"].rearrange("(f a) -> f a", a=1)),
                   (battb[:, :], a["L1_gnn_b_att"].partition_broadcast(P)),
                   (wq1[:, :], a["L2_gnn_Wq1"]), (wv1[:, :], a["L2_gnn_Wv1"]), (ws1[:, :], a["L2_gnn_Ws1"]),
                   (rows3[:, 0, :], a["L3_gnn_ln_gamma"].partition_broadcast(P)),
                   (rows3[:, 1, :], a["L3_gnn_ln_beta"].partition_broadcast(P)),
                   (rows3[:, 2, :], a["L3_gnn_b"].partition_broadcast(P)),
                   (rows3[:, 3, :], a["L1_gnn_b_lin"].partition_broadcast(P))]
            for h in range(4):
                wts.append((wkT[:, h, 128:129], a["L2_gnn_bk1"][h * F:(h + 1) * F].rearrange("(f a) -> f a", a=1)))
                wts.append((bq1T[:, h:h + 1], a["L2_gnn_bq1"][h * F:(h + 1) * F].rearrange("(f a) -> f a", a=1)))
                wts.append((bs1T[:, h:h + 1], a["L2_gnn_bs1"][h * F:(h + 1) * F].rearrange("(f a) -> f a", a=1)))
                wts.append((bv4[h:h + 1, h, :], a["L2_gnn_bv1"][h * F:(h + 1) * F].rearrange("(a f) -> a f", a=1)))
            assert len(wts) == NWT
            for dst_t, w in wts:
                sp.dma_start(dst_t, w).then_inc(s_wt, 16)
            for o in (0, 1):
                sp.wait_ge(s_pad, 1)
                sp.dma_start(rec_dram[o].rearrange("(p t) w -> p (t w)", p=P), fill[o]).then_inc(s_filled, 16)
            with sp.Fori(0, CH) as i:
                sp.wait_ge(ph("n0_evac"), i + 2)
                sp.dma_start(table_rows(t_v0, i), vs).then_inc(ph("n0_table"), 16)
                sp.wait_ge(ph("n0_table"), i * 16 + 16)
                sp.sem_inc(ph("n0_stored"), 1)

            def records_back(o):
                sp.wait_ge(s_scd, o + 1)
                sp.dma_start(rec[o][:, :, :].rearrange("p t w -> p (t w)"),
                             rec_dram[o].rearrange("(p t) w -> p (t w)", p=P)[:, 0:T * RW[o]]).then_inc(s_rec, 16)

            def rel_rows_out(o):
                sp.wait_ge(s_rele, (o + 1))
                sp.dma_start(relT_dram[o].rearrange("(q r) e -> r q e", q=4), relTs[0:TQ, :, :]).then_inc(s_relw, 16)

            records_back(0)
            rel_rows_out(0)
            sp.wait_ge(ph("L0h1_kept"), 1)
            sp.dma_start(t_v1.rearrange("(b p) f -> p b f", p=P), acc[:, :, 64:129]).then_inc(ph("v1_table"), 16)
            def rel_rows(name, o):
                credit(sp, name, "_ohT", 2)
                with sp.Fori(0, G) as i:
                    for h in (0, 1):
                        sp.wait_ge(sig(name, "_ohT"), nth(name, i) * 2 + h + 1)
                        rows = relT_dram[o][ds(i * U + h * HU, HU), :].rearrange("t e -> (t e)")
                        sp.dma_start(relB[:, h, :], rows.partition_broadcast(P)).then_inc(s_relB[h], 16)

            def node_table(name, table, tile):
                with sp.Fori(0, CH) as i:
                    sp.wait_ge(sig(name, "_filled"), i + 1)
                    sp.dma_start(table_rows(table, i), tile).then_inc(sig(name, "_table"), 16)
                    sp.wait_ge(sig(name, "_table"), nth(name, i) * 16 + 16)
                    sp.sem_inc(sig(name, "_stored"), 1)

            sp.wait_ge(ph("n1_done"), 1)
            sp.dma_start(t_sj.rearrange("(b p) f -> p b f", p=P), node1[:, :, 12:16]).then_inc(ph("sj_table"), 16)
            sp.dma_start(t_xl.rearrange("(b p) f -> p b f", p=P)[:, :, 0:F], xl).then_inc(ph("xl_table"), 16)
            rel_rows("L1B", 0)
            records_back(1)
            sp.wait_ge(ph("n1_sums"), 1)
            sp.dma_start(t_xl.rearrange("(b p) f -> p b f", p=P)[:, :, F:F + 12], node1[:, :, 0:12]).then_inc(ph("xl_table"), 16)
            rel_rows_out(1)
            sp.wait_ge(s_relw, 32)
            rel_rows("L1C", 1)
            sp.wait_ge(ph("L1C_kept"), 1)
            sp.dma_start(wk1, a["L2_gnn_Wk1"]).then_inc(ph("wraw"), 16)
            sp.dma_start(w3, a["L3_gnn_W"]).then_inc(ph("wraw"), 16)
            node_table("n2", t_h2, hs)
            rel_rows("L2Aq", 1)
            sp.wait_ge(ph("values_ready"), 1)
            rel_rows("L2C", 1)
            sp.wait_ge(ph("L2C_kept"), 1)
            for n, (c, nm) in enumerate(((0, "q"), (256, "k"), (512, "v"), (768, "s"))):
                w = 128 if nm == "s" else 256
                sp.dma_start(wl2[:, :, c:c + w], a[f"L2_gnn_W{nm}2"].rearrange("(h p) f -> p h f", p=P)).then_inc(ph("wl2"), 16)
                sp.dma_start(bl2[:, c:c + w], a[f"L2_gnn_b{nm}2"].partition_broadcast(P)).then_inc(ph("wl2"), 16)
            with sp.Fori(0, CH) as i:
                sp.wait_ge(ph("n2b_filled"), i + 1)
                sp.dma_start(table_rows(t_k2, i), kv[:, :, 0:256]).then_inc(ph("n2b_table"), 16)
                sp.dma_start(table_rows(t_v2, i), kv[:, :, 256:512]).then_inc(ph("n2b_table"), 16)
                sp.wait_ge(ph("n2b_table"), i * 32 + 32)
                sp.sem_inc(ph("n2b_stored"), 1)
            rel_rows("L2Dq", 1)
            sp.wait_ge(ph("values_ready"), 2)
            rel_rows("L2F", 1)
            node_table("n3", t_h3, vs)
            sp.wait_ge(ph("final"), 1)
            sp.dma_start(out[0:NFULL * P, :].rearrange("(b p) f -> p b f", p=P), x[:, 0:NFULL, :]).then_inc(s_out, 16)
            sp.dma_start(out[NFULL * P:N, :], x[0:NREST, NFULL, :]).then_inc(s_out, 16)
            sp.wait_ge(s_out, 32)
            for o in (0, 1):
                sp.wait_ge(s_relw, (o + 1) * 16)

        @block.gpsimd
        def _(pool):
            nc.gpsimd.memset(ident[:, :], 0.0).then_inc(s_cst, 1)
            nc.gpsimd.memset(lower, 1.0).then_inc(s_cst, 1)
            nc.gpsimd.iota(iota_f[:, :], [[1, P]], base=0, channel_multiplier=0, allow_small_or_imprecise_dtypes=True).then_inc(s_cst, 1)
            nc.gpsimd.iota(pidx[:, :], [[0, 1]], base=0, channel_multiplier=1, allow_small_or_imprecise_dtypes=True).then_inc(s_cst, 1)
            nc.gpsimd.iota(bval, [[1, KB]], base=0, channel_multiplier=0, allow_small_or_imprecise_dtypes=True).then_inc(s_cst, 1)
            nc.gpsimd.iota(iotaT, [[1, T]], base=0, channel_multiplier=0, allow_small_or_imprecise_dtypes=True).then_inc(s_cst, 1)
            nc.gpsimd.memset(ones, 1.0).then_inc(s_cst, 1)
            pool.wait_ge(s_cst, 7)
            nc.gpsimd.affine_select(out=ident[:, :], in_=ident[:, :], compare_op=ALU.not_equal, fill=1.0,
                                    base=0, pattern=[[-1, P]], channel_multiplier=1).then_inc(s_cst, 1)
            nc.gpsimd.affine_select(out=lower, in_=lower, compare_op=ALU.is_gt, fill=0.0,
                                    base=0, pattern=[[1, P]], channel_multiplier=-1).then_inc(s_cst, 1)

            SG = J // U

            def scatter(o, start, end):
                if start == 0:
                    pool.wait_ge(s_pos, (o + 1))
                    pool.sem_inc(s_gate, 1)
                    pool.wait_ge(s_filled, 32)
                    pool.sem_inc(s_gate, 1)

                def body(i, first):
                    for h in (0, 1):
                        j = i * U + h * HU
                        if not first:
                            pool.wait_ge(s_sc[h], (i + o * SG) * HU * 16)
                            pool.sem_inc(s_gate, 1)
                        nc.gpsimd.tensor_copy(sc_idx[:, h * HU:(h + 1) * HU], rowI[o][:, ds(j, HU)]).then_inc(s_cp, 1)
                        nc.gpsimd.tensor_copy(sc_rec[o][:, h * HU:(h + 1) * HU, :], recE[o][:, ds(j, HU), :]).then_inc(s_cp, 1)
                        pool.wait_ge(s_cp, (i + o * SG) * 4 + 2 * h + 2)
                        pool.sem_inc(s_gate, 1)
                        for k in range(h * HU, (h + 1) * HU):
                            nc.gpsimd.indirect_dma_start(
                                rec_dram[o], bass.IndirectOffsetOnAxis(ap=sc_idx[:, k:k + 1], axis=0),
                                sc_rec[o][:, k, :], None).then_inc(s_sc[h], 16)

                if start == 0:
                    body(0, o == 0)
                with pool.Fori(max(start, 1), end) as i:
                    body(i, False)
                if end == SG:
                    for h in (0, 1):
                        pool.wait_ge(s_sc[h], (o + 1) * SG * HU * 16)
                    pool.sem_inc(s_scd, 1)

            def gathers(name, o, table, width):
                col = ring
                used = sig(name, "_product" if name in SUMS else "_used")
                if name not in SUMS:
                    credit(pool, name, "_used", 2)
                with pool.Fori(0, G) as i:
                    for h in (0, 1):
                        pool.wait_ge(used, nth(name, i) * 2 + h + 1)
                        pool.sem_inc(s_gate, 1)
                        nc.gpsimd.tensor_copy(idx_slot[:, h * HU:(h + 1) * HU],
                                              rec[o][:, ds(i * U + h * HU, HU), 0].bitcast(i32)).then_inc(ph("indices"), 1)
                        pool.wait_ge(ph("indices"), (i + rounds[name] * G) * 2 + h + 1)
                        pool.sem_inc(s_gate, 1)
                        for k in range(h * HU, (h + 1) * HU):
                            nc.gpsimd.indirect_dma_start(
                                col[:, k, 0:width], None, table,
                                bass.IndirectOffsetOnAxis(ap=idx_slot[:, k:k + 1], axis=0)).then_inc(s_gath[k // QU], 16)

            scatter(0, 0, SG)
            pool.wait_ge(s_rec, 16)
            pool.sem_inc(s_gate, 1)
            pool.wait_ge(ph("n0_table"), CH * 16)
            pool.sem_inc(s_gate, 1)
            gathers("L0h1", 0, t_v0, 128)
            pool.wait_ge(ph("v1_table"), 16)
            pool.sem_inc(s_gate, 1)
            gathers("L0h2", 0, t_v1, 65)

            def table_ready(name, count):
                pool.wait_ge(ph(name), count)
                pool.sem_inc(s_gate, 1)

            PART = SG // 3
            scatter(1, 0, PART)
            table_ready("sj_table", 16)
            gathers("L1A", 0, t_sj, 4)
            scatter(1, PART, SG)
            table_ready("xl_table", 32)
            gathers("L1C", 1, t_xl, 140)
            table_ready("n2_table", 16 * CH)
            table_ready("n2_free", 1)
            gathers("L2A", 1, t_h2, F)
            table_ready("values_ready", 1)
            gathers("L2C", 1, t_h2, F)
            table_ready("n2b_table", 32 * CH)
            table_ready("n2b_free", 1)
            gathers("L2D", 1, t_k2, 256)
            table_ready("values_ready", 2)
            gathers("L2F", 1, t_v2, 256)
            table_ready("n3_table", 16 * CH)
            table_ready("n3_free", 1)
            gathers("L3", 1, t_h3, F)

        @block.vector
        def _(dve):
            V = nc.vector
            V.memset(kI, NP).then_inc(v_s[0], 1)
            V.memset(oI, NP).then_inc(v_s[0], 1)
            V.memset(wF, 0.0).then_inc(v_s[0], 1)
            V.memset(zeros, 0.0).then_inc(v_s[0], 1)
            V.memset(acc[:, 0:8, :].rearrange("p a b -> p (a b)"), 0.0).then_inc(v_s[0], 1)
            dve.wait_ge(v_s[0], 5)
            V.memset(bv4[:, :, :], 0.0)
            V.memset(fill[0].rearrange("p (t w) -> p t w", w=RW[0])[:, :, 1], -1.0)
            V.memset(fill[1].rearrange("p (t w) -> p t w", w=RW[1])[:, :, 1], -1.0).then_inc(s_pad, 1)
            V.memset(x[:, NFULL, :], 0.0).then_inc(s_xz, 1)
            V.memset(recE[0].rearrange("p j w -> p (j w)"), 0.0).then_inc(v_s[0], 1)
            V.memset(recE[1].rearrange("p j w -> p (j w)"), 0.0).then_inc(v_s[0], 1)

            def bucket(o, first):
                key, other = (kI, oI) if o == 0 else (oI, kI)
                s = Steps(dve, v_s[o], 0, 0, first)
                s.link(V.tensor_single_scalar(tI, key, 7, ALU.arith_shift_right))
                s.link(V.tensor_copy(blkF, tI))
                s.link(V.tensor_single_scalar(tI, key, P - 1, ALU.bitwise_and))
                s.link(V.tensor_copy(recE[o][:, :, 1], tI))
                s.link(V.tensor_copy(recE[o][:, :, 0].bitcast(i32), other))
                s.link(V.tensor_copy(recE[0][:, :, 2], wF) if o == 0 else V.memset(tmp, 0.0))
                s.link(V.memset(rank[o], 0.0))
                s.link(V.memset(mapF, 0.0))
                with dve.Fori(0, KB) as b:
                    l = Steps(dve, v_s[o], b, 5, s.start + s.n)
                    l.link(V.tensor_scalar(msk, blkF, bval[:, ds(b, 1)], None, ALU.is_equal))
                    l.link(V.tensor_tensor_scan(cum, msk, zeros, 0.0, ALU.add, ALU.max))
                    l.link(V.tensor_copy(cnt[:, ds(b, 1)], cum[:, J - 1:J]))
                    l.link(V.tensor_tensor(tmp, msk, cum, ALU.mult))
                    l.link(V.tensor_tensor(rank[o], rank[o], tmp, ALU.add))
                    l.end()
                s.n += KB * 5
                dve.wait_ge(s_pref, (o + 1))
                s.link(V.tensor_scalar(tilI, ps[:, 7, 0:KB], float(P - 1), None, ALU.add))
                s.link(V.tensor_single_scalar(tilI, tilI, 7, ALU.arith_shift_right))
                s.link(V.tensor_copy(til, tilI))
                s.link(V.tensor_tensor_scan(end_, til, zeros[:, 0:KB], 0.0, ALU.add, ALU.max))
                s.link(V.tensor_scalar(last_tile[o][:, :], end_, -1.0, 0.0, ALU.add, ALU.max))
                s.link(V.tensor_tensor(base, end_, til, ALU.subtract))
                s.link(V.memset(base[:, NB:KB], float(T)))
                s.link(V.tensor_scalar(base, base, float(P), -1.0, ALU.mult, ALU.add))
                s.link(V.tensor_tensor(base, base, ps[:, 6, 0:KB], ALU.add))
                with dve.Fori(0, KB) as b:
                    l = Steps(dve, v_s[o], b, 3, s.start + s.n)
                    l.link(V.tensor_scalar(tmp, blkF, bval[:, ds(b, 1)], base[:, ds(b, 1)], ALU.is_equal, ALU.mult))
                    l.link(V.tensor_tensor(rank[o], rank[o], tmp, ALU.add))
                    l.link(V.scalar_tensor_tensor(mapF, iotaT, end_[:, ds(b, 1)], mapF, ALU.is_ge, ALU.add))
                    l.end()
                s.n += KB * 3
                s.link(V.tensor_scalar(mapI[o], mapF, float(NB - 1), None, ALU.min))
                s.link(V.tensor_copy(tI, rank[o]))
                s.link(V.tensor_single_scalar(rowI[o], tI, P - 1, ALU.bitwise_and))
                s.link(V.tensor_copy(tmp, rowI[o]))
                s.link(V.tensor_single_scalar(tI, tI, 7, ALU.arith_shift_right))
                s.link(V.tensor_copy(tf, tI))
                V.scalar_tensor_tensor(rowI[o], tmp, float(TP), tf, ALU.mult, ALU.add).then_inc(s_pos, 1)
                dve.wait_ge(s_pos, (o + 1))
                return s.n

            def layer_norm(s, xin, root_ready):
                s.link(V.tensor_reduce(st[:, 0:CB], xin, AX, ALU.add))
                s.link(V.tensor_scalar(st[:, 8:8 + CB], st[:, 0:CB], 1.0 / F, None, ALU.mult))
                s.link(V.tensor_tensor(xc, xin, st[:, 8:8 + CB].unsqueeze(2).to_broadcast([P, CB, F]), ALU.subtract))
                s.link(V.tensor_tensor(sq, xc, xc, ALU.mult))
                s.link(V.tensor_reduce(st[:, 16:16 + CB], sq, AX, ALU.add))
                s.link(V.tensor_scalar(st[:, 24:24 + CB], st[:, 16:16 + CB], 1.0 / F, 1e-5, ALU.mult, ALU.add))
                root_ready()
                s.link(V.reciprocal(st[:, 40:40 + CB], st[:, 32:32 + CB]))
                s.link(V.tensor_tensor(hs, xc, st[:, 40:40 + CB].unsqueeze(2).to_broadcast([P, CB, F]), ALU.mult))

            def sweep_one_hots(name, o, weighted):
                with dve.Fori(0, G) as i:
                    for h in (0, 1):
                        dve.wait_ge(sig(name, "_product"), nth(name, i) * 2 + h + 1)
                        at = slice(h * HU, (h + 1) * HU)
                        rel = rec[o][:, ds(i * U + h * HU, HU), 1:2].to_broadcast([P, HU, P])
                        nodes = iota_f[:, :].unsqueeze(1).to_broadcast([P, HU, P])
                        if weighted:
                            V.tensor_tensor(ohm[:, at, :], rel, nodes, ALU.is_equal).then_inc(sig(name, "_plain"), 1)
                            dve.wait_ge(sig(name, "_plain"), nth(name, i) * 2 + h + 1)
                            w = rec[o][:, ds(i * U + h * HU, HU), 2:3].to_broadcast([P, HU, P])
                            V.tensor_tensor(oh[:, at, :], ohm[:, at, :], w, ALU.mult).then_inc(sig(name, "_onehot"), 1)
                        else:
                            V.tensor_tensor(oh[:, at, :], rel, nodes, ALU.is_equal).then_inc(sig(name, "_onehot"), 1)

            dve.wait_ge(s_key, 48)
            dve.wait_ge(s_cst, 9)
            dve.wait_ge(v_s[0], PRE)
            done = bucket(0, PRE)

            dve.wait_ge(s_x, 32)
            PER = NLN
            dve.sem_inc(ph("n0_transposed"), 1)
            with dve.Fori(0, CH) as i:
                s = Steps(dve, ph("n0_dve"), i, PER)
                dve.wait_ge(ph("n0_transposed"), i + 1)
                layer_norm(s, x[:, ds(i * CB, CB), :], lambda: dve.wait_ge(ph("n0_root"), i + 1))
                s.link(V.tensor_scalar(hs, hs, 0.0, None, ALU.max))
                s.end()
            bucket(1, 0)

            dve.wait_ge(s_rec, 16)
            V.tensor_copy(blk[0][:, :], mapI[0]).then_inc(s_relf, 1)
            V.tensor_copy(relF, rec[0][:, :, 1]).then_inc(s_relf, 1)
            dve.wait_ge(s_relf, 2)
            dve.wait_ge(ph("n0_table"), 16 * CH)
            dve.wait_ge(s_rele, 1)
            flow = Steps(dve, ph("flow"), 0, 0)
            link = flow.link
            link(V.tensor_copy(wrest, rec[0][:, :, 2]))
            for part in range(3):
                link(V.tensor_copy(w3b[:, :, part], wrest))
                if part < 2:
                    link(V.tensor_tensor(wrest, wrest, w3b[:, :, part], ALU.subtract))
            V.memset(zero_b, 0.0).then_inc(ph("sums_zero"), 1)
            sweep_one_hots("L0h1", 0, True)
            dve.wait_ge(sig("L0h1", "_closed"), nth("L0h1", G) // G)
            link(V.tensor_copy(acc[:, :, 0:F], psum_blocks))
            link(V.tensor_reduce(acc[:, :, 128], ps[:, 7, 0:3 * NB].rearrange("p (b c) -> p b c", c=3), AX, ALU.add))
            dve.sem_inc(ph("L0h1_kept"), 1)
            sweep_one_hots("L0h2", 0, True)
            dve.wait_ge(sig("L0h2", "_closed"), nth("L0h2", G) // G)
            link(V.tensor_copy(acc[:, :, 129:194], psum_blocks[:, :, 0:65]))

            dve.wait_ge(s_w0, 128)
            NE = 15
            with dve.Fori(0, CH) as i:
                for hop in (0, 1):
                    s = Steps(dve, ph("l0e_dve"), i, 2 * NE)
                    s.n = hop * NE
                    c0, dc = ((0, 128), (129, 193))[hop]
                    part = ds(i * CB, CB)
                    deg = acc[:, part, dc]
                    m, t, r = st[:, 0:CB], st[:, 8:8 + CB], st[:, 16:16 + CB]
                    z, g = st[:, 24:24 + CB], st[:, 32:32 + CB]
                    y, q, n = hs[:, :, 0:64], xc[:, :, 0:64], sq[:, :, 0:64]
                    s.link(V.tensor_scalar(m, deg, 0.0, None, ALU.is_gt))
                    s.link(V.tensor_tensor(t, deg, m, ALU.mult))
                    s.link(V.tensor_scalar(r, m, -1.0, 1.0, ALU.mult, ALU.add))
                    s.link(V.tensor_tensor(t, t, r, ALU.add))
                    s.link(V.reciprocal(r, t))
                    s.link(V.tensor_tensor(r, r, m, ALU.mult))
                    s.link(V.tensor_tensor(y, acc[:, part, c0:c0 + 64], r.unsqueeze(2).to_broadcast([P, CB, 64]), ALU.mult))
                    s.link(V.tensor_tensor(y, y, brow[:, 0:1, hop * 64:hop * 64 + 64].to_broadcast([P, CB, 64]), ALU.add))
                    s.link(V.tensor_tensor(q, y, brow[:, 1:2, hop * 64:hop * 64 + 64].to_broadcast([P, CB, 64]), ALU.mult))
                    s.link(V.tensor_reduce(z, q, AX, ALU.add))
                    s.link(V.tensor_scalar(n, y, 0.0, None, ALU.min))
                    dve.wait_ge(ph("l0e_gate"), i * 2 + hop + 1)
                    s.link(V.tensor_tensor(n, n, g.unsqueeze(2).to_broadcast([P, CB, 64]), ALU.mult))
                    s.link(V.tensor_scalar(y, y, 0.0, None, ALU.max))
                    s.link(V.tensor_tensor(y, y, n, ALU.add))
                    xp = x[:, part, hop * 64:hop * 64 + 64]
                    s.link(V.tensor_tensor(xp, xp, y, ALU.add))
            def bc(v, n):
                return v.unsqueeze(len(v.shape)).to_broadcast(list(v.shape) + [n])

            def split(link, parts, value):
                for n in range(3):
                    link(V.tensor_copy(parts[n], value))
                    if n < 2:
                        link(V.tensor_tensor(value, value, parts[n], ALU.subtract))

            def lookup_one_hots(name, i, h, dst):
                dve.wait_ge(s_relB[h], (i + rel_rounds[name] * G) * 16 + 16)
                V.tensor_scalar(dst, relB[:, h, :], pidx[:, 0:1], None, ALU.is_equal).then_inc(sig(name, "_ohT"), 1)

            def prepare(name, o, i, h):
                dve.wait_ge(s_relB[h], (i + rel_rounds[name] * G) * 16 + 16)
                dve.wait_ge(sig(name, "_looked"), nth(name, i) * 2 + h + 1)
                V.tensor_scalar(ohTb[:, h, :], relB[:, h, :], pidx[:, 0:1], None, ALU.is_equal).then_inc(sig(name, "_ohT"), 1)
                dve.wait_ge(sig(name, "_product"), nth(name, i) * 2 + h + 1)
                V.tensor_tensor(ohm[:, h * HU:(h + 1) * HU, :],
                                rec[o][:, ds(i * U + h * HU, HU), 1:2].to_broadcast([P, HU, P]),
                                iota_f[:, :].unsqueeze(1).to_broadcast([P, HU, P]), ALU.is_equal).then_inc(sig(name, "_onehot"), 1)

            def looked_up(name, i, h, width, looked=looked, bank=7):
                v = looked[:, h, 0:HU * width].rearrange("p (k f) -> p k f", f=width)
                dve.wait_ge(sig(name, "_looked"), nth(name, i) * 2 + h + 3)
                V.tensor_reduce(v, ps[:, bank, 0:HU * 3 * width].rearrange("p (k c f) -> p k f c", c=3, f=width), AX,
                                ALU.add).then_inc(sig(name, "_read"), 1)
                dve.wait_ge(sig(name, "_read"), nth(name, i) * 2 + h + 2)
                return v

            def max_constants(H):
                link(V.tensor_scalar(low_id, ident[:, :], -BIG, None, ALU.mult))
                rI = rowno[:, 1:2].bitcast(i32)
                link(V.tensor_copy(rI, pidx[:, 0:1]))
                link(V.tensor_single_scalar(rI, rI, H - 1, ALU.bitwise_and))
                link(V.tensor_copy(rowno[:, 0:1], rI))
                link(V.tensor_scalar(of_head[:, 0:H], iota_f[:, 0:H], rowno[:, 0:1], None, ALU.is_equal))
                link(V.tensor_copy(rI, pidx[:, 0:1]))
                link(V.tensor_single_scalar(rI, rI, HU * H - 1, ALU.bitwise_and))
                link(V.tensor_single_scalar(rI, rI, H.bit_length() - 1, ALU.arith_shift_right))
                link(V.tensor_copy(rowno[:, 0:1], rI))
                link(V.tensor_scalar(pick, iota_f[:, 0:HU].unsqueeze(2).to_broadcast([P, HU, P]), rowno[:, 0:1], None,
                                     ALU.is_equal))
                dve.sem_inc(ph("max_constants"), 1)

            def sweep_maxima(name, o):
                H = heads[name]
                nq = name + "q"
                NS = 6
                base = nth(name, 0) * NS * 2

                def score(s, i, h, k):
                    t = h * HU + k
                    if t % QU == 0:
                        dve.wait_ge(s_gath[t // QU], (i + rounds[name] * G) * QU * 16 + QU * 16)
                    dve.wait_ge(sig(nq, "_q"), nth(nq, i) * U + t + 1)
                    q = ps[:, k % 4, 0:H * P].rearrange("p (h c) -> p h c", h=H)
                    g = ring[:, t, 0:F].unsqueeze(1).to_broadcast([P, H, F]) if H == 4 else \
                        ring[:, t, 0:H * F].rearrange("p (h c) -> p h c", h=H)
                    V.tensor_tensor(q, q, g, ALU.mult).then_inc(sig(nq, "_multiplied"), 1)

                def reduce_max(i, h, k):
                    dve.wait_ge(sig(name, "_maxed"), nth(name, i) * U + h * HU + k + 1)
                    V.tensor_reduce(tile_mx[:, ds(i * U + h * HU + k, 1), 0:H].rearrange("p a h -> p (a h)"),
                                    ps[:, 4 + k % 2, 0:H * P].rearrange("p (h e) -> p h e", h=H), AX,
                                    ALU.max).then_inc(sig(name, "_reduced"), 1)

                def half(i, h, first, last):
                    at = slice(h * HU, (h + 1) * HU)
                    s = Steps(dve, sig(name, "_dve"), i, 2 * NS, base)
                    s.n = h * NS
                    if name != "L1A":
                        if first:
                            one_hots_q(i, h)
                    if name == "L1A":
                        for t in (h * HU, h * HU + QU):
                            dve.wait_ge(s_gath[t // QU], (i + rounds[name] * G) * QU * 16 + QU * 16)
                        s.link(V.tensor_copy(aS[:, at, :], ring[:, at, 0:4]))
                        dve.sem_inc(sig(name, "_used"), 1)
                    for k in range(HU):
                        if name != "L1A":
                            score(s, i, h, k)
                            if k < 3 and not (isinstance(i, int) and i == 0):
                                reduce_max(i - 1, h, k + 5)
                        if k >= 3 and not first:
                            reduce_max(*before(i, h), k - 3)
                        if k == 2 and name != "L1A" and not last:
                            one_hots_q(*((i, 1) if h == 0 else (i + 1, 0)))
                        if k == (0 if name == "L1A" else 4):
                            V.tensor_tensor(ohm[:, at, :], rec[o][:, ds(i * U + h * HU, HU), 1:2].to_broadcast([P, HU, P]),
                                            iota_f[:, :].unsqueeze(1).to_broadcast([P, HU, P]), ALU.not_equal)\
                                .then_inc(sig(name, "_masks"), 1)
                    if name == "L1A" and not first:
                        for k in range(5, HU):
                            reduce_max(*before(i, h), k)
                    if name != "L1A":
                        dve.wait_ge(sig(nq, "_summed"), nth(nq, i) * U + 4 + (h + 1) * HU)
                        dve.sem_inc(sig(name, "_used"), 1)
                    if name == "L2A":
                        pl = looked_up(nq, i, h, 4, lookedQ)
                        s.link(V.tensor_tensor(aS[:, at, :], aS[:, at, :], pl, ALU.add))
                    kept = V.tensor_copy(alpha[:, ds(i * U + h * HU, HU), 0:H], aS[:, at, 0:H])
                    if name == "L2D":
                        s.did(kept)
                    w = HU * H
                    split(s.link, [score3[:, h, c * w:(c + 1) * w].rearrange("p (k h) -> p k h", h=H) for c in range(3)],
                          aS[:, at, 0:H])

                def one_hots_q(i, h):
                    if name == "L2A":
                        dve.wait_ge(s_relB[h], (i + rel_rounds[name] * G) * 16 + 16)
                        V.tensor_scalar(ohTq[:, h, :], relB[:, h, :], pidx[:, 0:1], None, ALU.is_equal)
                    lookup_one_hots(nq, i, h, ohT[:, h, :])

                passes(dve, half)
                if name != "L1A":
                    for k in range(5, HU):
                        reduce_max(G - 1, 0, k)
                for k in range(HU):
                    reduce_max(G - 1, 1, k)
                dve.wait_ge(sig(name, "_reduced"), nth(name, G) * U + 2)
                link(V.memset(starts[:, 0:1], 0.0))
                link(V.tensor_tensor(starts[:, 1:T], blk[o][:, 1:T], blk[o][:, 0:T - 1], ALU.not_equal))
                link(V.tensor_scalar(starts, starts, -BIG, None, ALU.mult))
                for hd in range(H):
                    link(V.tensor_tensor_scan(run_mx[:, :, hd], starts, tile_mx[:, :, hd], -BIG, ALU.add, ALU.max))
                with dve.Fori(0, NB // 5) as c:
                    tiles = nc.values_load_multi_w_load_instructions(
                        last_tile[o][0:1, ds(c * 5, 5)], engines=[mybir.EngineType.DVE], min_val=0, max_val=T - 1,
                        skip_runtime_bounds_check_because="the sort takes the maximum with 0, and all blocks end before tile T")[1]
                    for n, t in enumerate(tiles):
                        V.tensor_copy(mx[:, ds(c * 5 + n, 1), 0:H], run_mx[:, ds(t, 1), 0:H]).then_inc(ph("block_maxima"), 1)
                dve.wait_ge(ph("block_maxima"), (MAXES.index(name) + 1) * NB)

            link(V.tensor_copy(ident_b[:, :], ident[:, :]))
            dve.wait_ge(s_wt, NWT * 16)
            dve.sem_inc(ph("n1_transposed"), 1)
            N1 = NLN + 3
            with dve.Fori(0, CH) as i:
                s = Steps(dve, ph("n1_dve"), i, N1)
                dve.wait_ge(ph("n1_transposed"), i + 1)
                layer_norm(s, x[:, ds(i * CB, CB), :], lambda: dve.wait_ge(ph("n1_root"), i + 1))
                s.link(V.tensor_scalar(hs, hs, 0.0, None, ALU.max))
                dve.wait_ge(ph("n1_mm"), i + 1)
                s.link(V.tensor_tensor(xl[:, ds(i * CB, CB), :], psf[:, 1024:1024 + CN].rearrange("p (b f) -> p b f", f=F),
                                       rows3[:, 3:4, :].to_broadcast([P, CB, F]), ALU.add))
                dve.wait_ge(ph("n1_att"), i + 1)
                pa = psf[:, 3072:3072 + CB * 8].rearrange("p (b f) -> p b f", f=8)
                s.link(V.tensor_tensor(node1[:, ds(i * CB, CB), 0:4], pa[:, :, 0:4],
                                       battb[:, :].unsqueeze(1).to_broadcast([P, CB, 4]), ALU.add))
                s.link(V.tensor_copy(node1[:, ds(i * CB, CB), 12:16], pa[:, :, 4:8]))
                s.end()
            V.memset(pE[:, :, :, :], 1.0).then_inc(ph("n1_done"), 1)
            dve.wait_ge(ph("n1_done"), 1)

            max_constants(4)
            sweep_maxima("L1A", 0)
            link(V.tensor_tensor(node1[:, :, 4:8], node1[:, :, 0:4], mx[:, :, :], ALU.add))
            link(V.scalar_tensor_tensor(node1[:, :, 4:8], node1[:, :, 4:8], 0.2, node1[:, :, 4:8], ALU.mult, ALU.max))

            link(V.tensor_copy(rest, node1[:, :, 0:8]))
            split(link, [node24[:, :, c, :] for c in range(3)], rest)
            link(V.tensor_copy(rest[:, :, 0:4], node1[:, :, 12:16]))
            split(link, [node12[:, :, c, :] for c in range(3)], rest[:, :, 0:4])
            link(V.memset(zero_b, 0.0))
            V.memset(p3[:, :, :], 1.0).then_inc(ph("L1B_tables"), 1)
            dve.wait_ge(ph("L1B_tables"), 1)

            def weights_b(i, h):
                s = Steps(dve, ph("L1B_dve"), i, 16)
                s.n = 8 * h
                z = zE[:, h, :, :]
                pl = looked_up("L1B", i, h, 8)
                s.link(V.tensor_tensor(z, alpha[:, ds(i * U + h * HU, HU), :], pl[:, :, 0:4], ALU.add))
                s.link(V.scalar_tensor_tensor(z, z, 0.2, z, ALU.mult, ALU.max))
                s.link(V.tensor_tensor(z, z, pl[:, :, 4:8], ALU.subtract))
                dve.wait_ge(sig("L1B", "_exp"), nth("L1B", i) * 2 + h + 1)
                at = slice(h * HU, (h + 1) * HU)
                split(s.link, [p3[:, at, 4 * c:4 * c + 4] for c in range(3)], pE[:, h, :, 0:4])

            ahead(dve, lambda i, h: prepare("L1B", 0, i, h), weights_b)
            dve.wait_ge(ph("L1B_closed"), 1)
            pb = ps[:, 4, 0:13 * NB].rearrange("p (b c) -> p b c", c=13)
            link(V.tensor_reduce(sums[:, :, 0:4], pb[:, :, 0:12].rearrange("p b (c f) -> p b f c", c=3), AX, ALU.add))
            link(V.tensor_copy(sums[:, :, 4], pb[:, :, 12]))
            link(V.tensor_scalar(node1[:, :, 8:12], sums[:, :, 0:4], 1e-16, None, ALU.add))
            V.reciprocal(node1[:, :, 8:12], node1[:, :, 8:12]).then_inc(ph("n1_sums"), 1)
            dve.wait_ge(ph("n1_sums"), 1)
            dve.wait_ge(s_rec, 32)
            dve.wait_ge(s_rele, 1)
            V.tensor_copy(blk[1][:, :], mapI[1]).then_inc(s_relf, 1)
            V.tensor_copy(relF, rec[1][:, :, 1]).then_inc(s_relf, 1)
            dve.wait_ge(s_relf, 4)

            def messages(i, h):
                s = Steps(dve, ph("L1C_dve"), i, 10)
                s.n = 5 * h
                pl = looked_up("L1C", i, h, 4)
                for k in (h * HU, h * HU + QU):
                    dve.wait_ge(s_gath[k // QU], (i + rounds["L1C"] * G) * QU * 16 + QU * 16)
                z = zE[:, h, :, :]
                g = ring[:, h * HU:(h + 1) * HU, :]
                s.link(V.tensor_tensor(z, g[:, :, 128:132], pl, ALU.add))
                s.link(V.scalar_tensor_tensor(z, z, 0.2, z, ALU.mult, ALU.max))
                s.link(V.tensor_tensor(z, z, g[:, :, 132:136], ALU.subtract))
                dve.wait_ge(sig("L1C", "_exp"), nth("L1C", i) * 2 + h + 1)
                s.link(V.tensor_tensor(z, pE[:, h, :, 0:4], g[:, :, 136:140], ALU.mult))
                m = g[:, :, 0:F].rearrange("p k (h c) -> p k h c", h=4)
                s.link(V.tensor_tensor(m, m, bc(z, 32), ALU.mult))

            ahead(dve, lambda i, h: prepare("L1C", 1, i, h), messages)
            dve.wait_ge(ph("L1C_closed"), 1)
            dve.wait_ge(ph("xl_table"), 32)
            link(V.tensor_copy(deg_in[:, :], ps[:, 6, F:F + NB]))
            link(V.tensor_scalar(tmN[:, :], deg_in[:, :], 0.0, None, ALU.is_equal))
            link(V.tensor_tensor(xl, xl, bc(tmN[:, :], F), ALU.mult))
            link(V.tensor_tensor(x[:, :, :], x[:, :, :], psum_blocks, ALU.add))
            link(V.tensor_tensor(x[:, :, :], x[:, :, :], xl, ALU.add))
            dve.sem_inc(ph("L1C_kept"), 1)

            dve.sem_inc(ph("n2_transposed"), 1)
            dve.sem_inc(ph("n2_stored"), 1)
            N2 = NLN + 16
            with dve.Fori(0, CH) as i:
                s = Steps(dve, ph("n2_dve"), i, N2)
                dve.wait_ge(ph("n2_transposed"), i + 1)
                dve.wait_ge(ph("n2_stored"), i + 1)
                layer_norm(s, x[:, ds(i * CB, CB), :], lambda: dve.wait_ge(ph("n2_root"), i + 1))
                s.did(V.tensor_scalar(hs, hs, 0.0, None, ALU.max))
                dve.wait_ge(ph("n2_dve"), s.start + s.n)
                dve.sem_inc(ph("n2_filled"), 1)
                for h in range(4):
                    dve.wait_ge(ph("n2_qk"), i * 4 + h + 1)
                    for c, (b0, nb) in enumerate(((0, 3), (3, 2))):
                        pv = ps[:, 6 + c, 0:nb * 129].rearrange("p (b f) -> p b f", f=129)
                        s.did(V.tensor_copy(big[:, ds(i * CB + b0, nb), h * F:(h + 1) * F], pv[:, :, 0:F]))
                        s.did(V.tensor_copy(node1[:, ds(i * CB + b0, nb), h:h + 1], pv[:, :, F:F + 1]))
                s.end()
            dve.wait_ge(ph("n2_dve"), CH * N2)
            link(V.tensor_copy(rest[:, :, 0:4], node1[:, :, 0:4]))
            split(link, [node12[:, :, c, :] for c in range(3)], rest[:, :, 0:4])
            max_constants(4)
            dve.sem_inc(ph("n2_free"), 1)

            def sweep_values(name):
                H = heads[name]
                base = nth(name, 0) * 12
                link(V.memset(accf, 0.0))
                link(V.tensor_copy(mrest[:, :, 0:H], mx[:, :, 0:H]))
                split(link, [mx12[:, :, c * H:(c + 1) * H] for c in range(3)], mrest[:, :, 0:H])
                link(V.memset(zero_b, 0.0))
                dve.sem_inc(ph("values_ready"), 1)

                def minus_maxima(i, h):
                    get_ready(i, h)
                    at = slice(h * HU, (h + 1) * HU)
                    s = Steps(dve, sig(name, "_dve"), i, 12, base)
                    s.n = 6 * h
                    dve.wait_ge(sig(name, "_onehot"), nth(name, i) * 2 + h + 1)
                    V.tensor_copy(oh[:, at, :], ohm[:, at, :]).then_inc(sig(name, "_wide"), 1)
                    pl = looked_up(name, i, h, H, bank=6)
                    s.link(V.tensor_tensor(zE[:, h, :, 0:H], alpha[:, ds(i * U + h * HU, HU), 0:H], pl, ALU.subtract))

                def in_parts(i, h):
                    at = slice(h * HU, (h + 1) * HU)
                    s = Steps(dve, sig(name, "_dve"), i, 12, base)
                    s.n = 6 * h + 1
                    dve.wait_ge(sig(name, "_exp"), (nth(name, i) * 2 + h) * 2 + 1)
                    split(s.link, [p3[:, at, c * H:(c + 1) * H] for c in range(3)], pE[:, h, :, 0:H])

                def add_up(i, h, nxt):
                    blocks = loaded_blocks(mybir.EngineType.DVE, 1, i, h)
                    for k in range(h * HU, (h + 1) * HU):
                        if nxt and k % HU == 3:
                            minus_maxima(*nxt)
                        if nxt and k % HU == 6:
                            in_parts(*nxt)
                        b = blocks[k % HU]
                        dve.wait_ge(sig(name, "_product"), nth(name, i) * U + k + 1)
                        dve.wait_ge(sig(name, "_added"), nth(name, i) * U + 4 + k)
                        part = acc[:, ds(b, 1), 0:H * P]
                        V.tensor_tensor(part, part, ps[:, k % 4, 0:H * P].unsqueeze(1), ALU.add).then_inc(sig(name, "_added"), 1)
                    dve.sem_inc(sig(name, "_used"), 1)

                def get_ready(i, h):
                    lookup_one_hots(name, i, h, ohTb[:, h, :])
                    V.tensor_tensor(ohm[:, h * HU:(h + 1) * HU, :],
                                    rec[1][:, ds(i * U + h * HU, HU), 1:2].to_broadcast([P, HU, P]),
                                    iota_f[:, :].unsqueeze(1).to_broadcast([P, HU, P]), ALU.is_equal)\
                        .then_inc(sig(name, "_onehot"), 1)

                minus_maxima(0, 0)
                in_parts(0, 0)
                with_next(dve, add_up)
                dve.wait_ge(sig(name, "_closed"), nth(name, G) // G)
                dve.wait_ge(sig(name, "_added"), nth(name, G) * U + 4)
                link(V.tensor_reduce(acc[:, :, 512:512 + H],
                                     ps[:, 7, 0:3 * H * NB].rearrange("p (b c f) -> p b f c", c=3, f=H), AX, ALU.add))
                dve.sem_inc(ph(name + "_kept"), 1)

            sweep_maxima("L2A", 1)
            sweep_values("L2C")

            dve.wait_ge(ph("wl2"), 128)
            link(V.tensor_scalar(wl2[:, :, 0:256], wl2[:, :, 0:256], ROOTD, None, ALU.mult))
            link(V.tensor_scalar(bl2[:, 0:256], bl2[:, 0:256], ROOTD, None, ALU.mult))
            dve.sem_inc(ph("wl2_scaled"), 1)
            dve.sem_inc(ph("n2b_stored"), 1)
            N2B = 4 + 3 * CB
            with dve.Fori(0, CH) as i:
                s = Steps(dve, ph("n2b_dve"), i, N2B)
                part = ds(i * CB, CB)
                r, f = stb[:, 0:CB, :], stb[:, CB:2 * CB, :]
                dve.wait_ge(ph("n2b_fl"), i + 1)
                s.link(V.tensor_scalar(f, acc[:, part, 512:516], 1e-16, None, ALU.add))
                s.link(V.reciprocal(r, f))
                s.link(V.tensor_tensor(f, acc[:, part, 512:516], r, ALU.mult))
                av = acc[:, part, 0:512].rearrange("p b (h c) -> p b h c", h=4)
                s.link(V.tensor_tensor(an, av, bc(r, F), ALU.mult))
                for b in range(CB):
                    dve.wait_ge(ph("n2b_mm"), (i * CB + b) + 1)
                    if b == 0:
                        dve.wait_ge(ph("n2b_stored"), i + 1)
                    pa, pb = ps[:, 6 * (b % 2), :], ps[:, 6 * (b % 2) + 1, :]
                    s.did(V.tensor_tensor(q2[:, ds(i * CB + b, 1), :], pa[:, 0:256].unsqueeze(1), bl2[:, 0:256].unsqueeze(1), ALU.add))
                    s.did(V.tensor_tensor(kv[:, b, 0:256], pa[:, 256:512], bl2[:, 256:512], ALU.add))
                    s.did(V.tensor_tensor(kv[:, b, 256:512], pb[:, 0:256], bl2[:, 512:768], ALU.add))
                    V.tensor_tensor(s2[:, ds(i * CB + b, 1), :], pb[:, 256:384].unsqueeze(1), bl2[:, 768:896].unsqueeze(1),
                                    ALU.add).then_inc(ph("n2b_evac"), 1)
                dve.wait_ge(ph("n2b_evac"), i * CB + CB + 2)
                dve.sem_inc(ph("n2b_filled"), 1)
                s.end()
            max_constants(2)
            dve.sem_inc(ph("n2b_free"), 1)
            sweep_maxima("L2D", 1)
            sweep_values("L2F")
            lN = mx[:, :, 0:2]
            link(V.tensor_scalar(lN, acc[:, :, 512:514], 1e-16, None, ALU.add))
            link(V.reciprocal(lN, lN))
            link(V.tensor_scalar(lN, lN, 0.5, None, ALU.mult))
            for h in (0, 1):
                part = acc[:, :, h * F:(h + 1) * F]
                link(V.tensor_tensor(part, part, bc(mx[:, :, h], F), ALU.mult))
                link(V.tensor_tensor(x[:, :, :], x[:, :, :], part, ALU.add))
            link(V.tensor_tensor(x[:, :, :], x[:, :, :], s2, ALU.add))

            link(V.tensor_scalar(sums[:, :, 3], sums[:, :, 4], 1.0, None, ALU.max))
            V.tensor_scalar(deg_in[:, :], deg_in[:, :], 1.0, None, ALU.max).then_inc(ph("deg_ready"), 1)
            dve.wait_ge(ph("deg_root"), 1)
            link(V.reciprocal(sums[:, :, 2], sums[:, :, 1]))
            link(V.reciprocal(sums[:, :, 3], sums[:, :, 0]))
            dve.sem_inc(ph("n3_transposed"), 1)
            dve.sem_inc(ph("n3_stored"), 1)
            N3 = 2 * NLN + 4
            with dve.Fori(0, CH) as i:
                s = Steps(dve, ph("n3_dve"), i, N3)
                part = ds(i * CB, CB)
                dve.wait_ge(ph("n3_transposed"), i + 1)
                dve.wait_ge(ph("n3_stored"), i + 1)
                layer_norm(s, x[:, part, :], lambda: dve.wait_ge(ph("n3_root"), i * 2 + 1))
                s.link(V.tensor_scalar(hs, hs, 0.0, None, ALU.max))
                layer_norm(s, hs, lambda: dve.wait_ge(ph("n3_root"), i * 2 + 2))
                s.link(V.tensor_tensor(hs, hs, rows3[:, 0:1, :].to_broadcast([P, CB, F]), ALU.mult))
                s.link(V.tensor_tensor(hs, hs, rows3[:, 1:2, :].to_broadcast([P, CB, F]), ALU.add))
                s.link(V.tensor_tensor(vs, hs, bc(sums[:, part, 2], F), ALU.mult))
                dve.sem_inc(ph("n3_filled"), 1)
                s.link(V.tensor_tensor(x[:, part, :], x[:, part, :], rows3[:, 2:3, :].to_broadcast([P, CB, F]), ALU.add))
                dve.wait_ge(ph("n3_mm"), i + 2)
                s.link(V.tensor_tensor(x[:, part, :], x[:, part, :],
                                       psf[:, 1024:1024 + CN].rearrange("p (b f) -> p b f", f=F), ALU.add))
                s.end()
            dve.sem_inc(ph("n3_free"), 1)
            V.memset(zero_b, 0.0).then_inc(ph("sums_zero"), 1)
            sweep_one_hots("L3", 1, False)
            dve.wait_ge(sig("L3", "_closed"), nth("L3", G) // G)
            link(V.tensor_copy(acc[:, :, 0:F], psum_blocks))
            dve.sem_inc(ph("n4_transposed"), 1)
            with dve.Fori(0, CH) as i:
                s = Steps(dve, ph("n4_dve"), i, 2)
                part = ds(i * CB, CB)
                dve.wait_ge(ph("n4_transposed"), i + 1)
                s.link(V.tensor_tensor(hs, acc[:, part, 0:F], bc(sums[:, part, 3], F), ALU.mult))
                dve.wait_ge(ph("n4_mm"), i + 2)
                s.link(V.tensor_tensor(x[:, part, :], x[:, part, :],
                                       psf[:, 1024:1024 + CN].rearrange("p (b f) -> p b f", f=F), ALU.add))
                s.end()
            dve.sem_inc(ph("final"), 1)

        @block.scalar
        def _(act):
            A = nc.scalar
            act.sem_inc(ph("n0_mm"), 1)
            act.sem_inc(ph("n0_stored"), 1)
            with act.Fori(0, CH) as i:
                act.wait_ge(ph("n0_dve"), i * NLN + VAR)
                A.activation(st[:, 32:32 + CB], st[:, 24:24 + CB], ACT.Sqrt).then_inc(ph("n0_root"), 1)
                act.wait_ge(ph("n0_transposed"), i + 2)
                act.wait_ge(ph("n0_mm"), i + 1)
                A.activation(hT, psf[:, 0:CN], ACT.Copy).then_inc(ph("n0_hT"), 1)
                act.wait_ge(ph("n0_mm"), i + 2)
                act.wait_ge(ph("n0_stored"), i + 1)
                A.activation(vs.rearrange("p b f -> p (b f)"), psf[:, 1024:1024 + CN], ACT.Copy).then_inc(ph("n0_evac"), 1)

            def rel_evac(o):
                act.wait_ge(s_relp, (o + 1))
                A.activation(relTs[0:TQ, :, :].rearrange("p q e -> p (q e)"), ps[0:TQ, 7, :], ACT.Copy).then_inc(s_rele, 1)

            rel_evac(0)
            act.wait_ge(s_w0, 128)
            with act.Fori(0, CH) as i:
                for hop in (0, 1):
                    act.wait_ge(ph("l0e_dve"), i * 30 + hop * 15 + 10)
                    A.activation(st[:, 32:32 + CB], st[:, 24:24 + CB], ACT.Sigmoid,
                                 bias=bf_b[:, hop:hop + 1]).then_inc(ph("l0e_gate"), 1)

            act.wait_ge(s_wt, NWT * 16)
            act.sem_inc(ph("n1_xlT"), 1)
            with act.Fori(0, CH) as i:
                act.wait_ge(ph("n1_dve"), i * (NLN + 3) + VAR)
                A.activation(st[:, 32:32 + CB], st[:, 24:24 + CB], ACT.Sqrt).then_inc(ph("n1_root"), 1)
                act.wait_ge(ph("n1_transposed"), i + 2)
                act.wait_ge(ph("n1_xlT"), i + 1)
                A.activation(hT, psf[:, 0:CN], ACT.Copy).then_inc(ph("n1_hT"), 1)
                act.wait_ge(ph("n1_xlT"), i + 2)
                A.activation(xlT, psf[:, 2048:2048 + CN], ACT.Identity, bias=blinT[:, 0:1]).then_inc(ph("n1_xlTe"), 1)

            def sweep_spread(name):
                H = heads[name]
                R3 = 3 * HU * H
                nq = name + "q"

                def spread_out(i, h):
                    act.wait_ge(sig(name, "_turned"), nth(name, i) * 2 + h + 1)
                    for hd in range(H):
                        ins = A.activation(spread[0:R3, h, hd * P:(hd + 1) * P], ps[0:R3, 6, 0:P], ACT.Copy,
                                           scale=of_head[0:R3, hd:hd + 1])
                    ins.then_inc(sig(name, "_spread"), 1)

                def half(i, h, first, last):
                    for k in range(HU):
                        if name != "L1A":
                            act.wait_ge(sig(nq, "_multiplied"), nth(nq, i) * U + h * HU + k + 1)
                            for hd in range(H):
                                q = ps[:, k % 4, hd * P:(hd + 1) * P]
                                ins = A.activation(q, q, ACT.Copy, accum_out=aS[:, h * HU + k, hd:hd + 1])
                            ins.then_inc(sig(nq, "_summed"), 1)
                        if k == 1 and not first:
                            spread_out(*before(i, h))

                passes(act, half)
                spread_out(G - 1, 1)

            sweep_spread("L1A")
            with act.Fori(0, G) as i:
                for h in (0, 1):
                    act.wait_ge(ph("L1B_dve"), i * 16 + h * 8 + 3)
                    A.activation(pE[:, h, :, 0:4], zE[:, h, :, :], ACT.Exp).then_inc(sig("L1B", "_exp"), 1)
            act.wait_ge(s_relw, 16)
            rel_evac(1)
            with act.Fori(0, G) as i:
                for h in (0, 1):
                    act.wait_ge(sig("L1C", "_onehot"), nth("L1C", i) * 2 + h + 1)
                    A.activation(oh[:, h * HU:(h + 1) * HU, :], ohm[:, h * HU:(h + 1) * HU, :], ACT.Copy).then_inc(ph("L1C_wide"), 1)
                    act.wait_ge(ph("L1C_dve"), i * 10 + h * 5 + 3)
                    A.activation(pE[:, h, :, 0:4], zE[:, h, :, :], ACT.Exp).then_inc(sig("L1C", "_exp"), 1)

            act.wait_ge(s_wT, 1)
            act.wait_ge(s_wt, NWT * 16)
            A.activation(wkT[:, :, 0:F], ps[:, 0, :].rearrange("p (h f) -> p h f", h=4), ACT.Copy)
            A.activation(bq1T[:, :], bq1T[:, :], ACT.Copy, scale=ROOTD)
            A.activation(w3T[:, :, :].rearrange("p a b -> p (a b)"), ps[:, 1, 0:256], ACT.Copy).then_inc(s_wTe, 1)
            act.wait_ge(s_wTe, 1)
            act.sem_inc(ph("n2_q"), 1)
            with act.Fori(0, CH) as i:
                act.wait_ge(ph("n2_dve"), i * (NLN + 16) + VAR)
                A.activation(st[:, 32:32 + CB], st[:, 24:24 + CB], ACT.Sqrt).then_inc(ph("n2_root"), 1)
                act.wait_ge(ph("n2_transposed"), i + 2)
                act.wait_ge(ph("n2_q"), i * 4 + 1)
                A.activation(hT, psf[:, 0:CN], ACT.Copy).then_inc(ph("n2_hT"), 1)
                A.activation(h2T[:, ds(i * CN, CN)], psf[:, 0:CN], ACT.Copy).then_inc(ph("n2_hT"), 1)
                for h in range(4):
                    act.wait_ge(ph("n2_q"), i * 4 + h + 2)
                    A.activation(qT[:, h % 2, :], psf[:, 1024 * (1 + h % 2):1024 * (1 + h % 2) + CN], ACT.Identity,
                                 bias=bq1T[:, h:h + 1], scale=ROOTD).then_inc(ph("n2_qT"), 1)

            def sweep_values(name):
                H = heads[name]
                credit(act, name, "_added", 4)

                def exponentials(i, h):
                    act.wait_ge(sig(name, "_dve"), (nth(name, i) * 2 + h) * 6 + 1)
                    A.activation(pE[:, h, :, 0:H], zE[:, h, :, 0:H], ACT.Exp).then_inc(sig(name, "_exp"), 1)
                    A.activation(pA[:, h, :, 0:H], zE[:, h, :, 0:H], ACT.Exp).then_inc(sig(name, "_exp"), 1)
                    act.wait_ge(sig(name, "_exp"), (nth(name, i) * 2 + h) * 2 + 2)

                def values(i, h, nxt):
                    for k in range(h * HU, (h + 1) * HU):
                        if nxt and k % HU == 5:
                            exponentials(*nxt)
                        act.wait_ge(sig(name, "_freed"), nth(name, i) * U + k + 1)
                        if k % QU == 0:
                            act.wait_ge(s_gath[k // QU], (i + rounds[name] * G) * QU * 16 + QU * 16)
                        for hd in range(H):
                            row = ring[:, k, 0:F] if H == 4 else ring[:, k, hd * F:(hd + 1) * F]
                            ins = A.activation(wide[:, k % 2, hd * P:(hd + 1) * P], row, ACT.Copy,
                                               scale=pA[:, h, k % HU, hd:hd + 1])
                        ins.then_inc(sig(name, "_value"), 1)

                exponentials(0, 0)
                with_next(act, values)

            sweep_spread("L2A")
            sweep_values("L2C")
            act.wait_ge(ph("wl2_scaled"), 1)
            with act.Fori(0, CH) as i:
                for h in range(4):
                    act.wait_ge(ph("n2b_aT"), i * 4 + h + 1)
                    A.activation(aT[:, h, :], psf[:, 0:CN], ACT.Copy).then_inc(ph("n2b_aTe"), 1)
                act.wait_ge(ph("n2b_fl"), i + 2)
                A.activation(flT[0:4, :], psf[0:4, 1024:1024 + CN], ACT.Copy).then_inc(ph("n2b_flT"), 1)
                for h in range(4):
                    act.wait_ge(ph("n2b_o"), i * 4 + h + 1)
                    A.activation(h1T[:, h, :], psf[:, 2048:2048 + CN], ACT.Relu, bias=bs1T[:, h:h + 1]).then_inc(ph("n2b_h1"), 1)
            sweep_spread("L2D")
            sweep_values("L2F")

            act.wait_ge(ph("deg_ready"), 1)
            A.activation(sums[:, :, 1], sums[:, :, 3], ACT.Sqrt)
            A.activation(sums[:, :, 0], deg_in[:, :], ACT.Sqrt).then_inc(ph("deg_root"), 1)
            act.sem_inc(ph("n3_mm"), 1)
            with act.Fori(0, CH) as i:
                for n in (0, 1):
                    act.wait_ge(ph("n3_dve"), i * (2 * NLN + 4) + n * NLN + VAR)
                    A.activation(st[:, 32:32 + CB], st[:, 24:24 + CB], ACT.Sqrt).then_inc(ph("n3_root"), 1)
                act.wait_ge(ph("n3_transposed"), i + 2)
                act.wait_ge(ph("n3_mm"), i + 1)
                A.activation(hT, psf[:, 0:CN], ACT.Copy).then_inc(ph("n3_hT"), 1)
            act.sem_inc(ph("n4_mm"), 1)
            with act.Fori(0, CH) as i:
                act.wait_ge(ph("n4_transposed"), i + 2)
                act.wait_ge(ph("n4_mm"), i + 1)
                A.activation(hT, psf[:, 0:CN], ACT.Copy).then_inc(ph("n4_hT"), 1)


        @block.tensor
        def _(pe):
            M = nc.tensor

            def prefix(o):
                pe.wait_ge(v_s[o], (PRE if o == 0 else 0) + 8 + KB * 5)
                M.matmul(ps[:, 6, 0:KB], lower, cnt, start=True, stop=True)
                M.matmul(ps[:, 7, 0:KB], ones, cnt, start=True, stop=True).then_inc(s_pref, 1)

            def rel_transpose(o):
                pe.wait_ge(s_relf, (o + 1) * 2)
                for q in range(4):
                    last = M.transpose(ps[0:TQ, 7, q * P:(q + 1) * P], relF[:, q * TQ:(q + 1) * TQ], ident[:, :])
                last.then_inc(s_relp, 1)

            def open_sums(banks, first, last_width=P):
                for bank in range(banks):
                    w = last_width if bank >= 6 else 512
                    last = M.matmul(ps[:, bank, 0:w], zero_b[:, 0:P], zero_b[:, 0:w], start=first, stop=not first)
                return last

            def sweep_sums(name, o, width, degrees=False):
                credit(pe, name, "_product", 2)
                banks = 8 if degrees else 7
                open_sums(banks, True)
                with pe.Fori(0, G) as i:
                    for h in (0, 1):
                        blocks = loaded_blocks(mybir.EngineType.PE, o, i, h)
                        pe.wait_ge(sig(name, "_onehot"), nth(name, i) * 2 + h + 1)
                        for k in range(h * HU, (h + 1) * HU):
                            b = blocks[k % HU]
                            if k % QU == 0:
                                pe.wait_ge(s_gath[k // QU], (i + rounds[name] * G) * QU * 16 + QU * 16)
                            if degrees:
                                M.matmul(ps[:, 7, ds(b * 3, 3)], ohm[:, k, :], w3b[:, ds(i * U + k, 1), :], start=False, stop=False)
                            ins = M.matmul(psum_blocks[:, ds(b, 1), 0:width], oh[:, k, :], ring[:, k, 0:width].unsqueeze(1),
                                           start=False, stop=False)
                        ins.then_inc(sig(name, "_product"), 1)
                open_sums(banks, False).then_inc(sig(name, "_closed"), 1)

            pe.wait_ge(s_cst, 9)
            prefix(0)
            pe.wait_ge(s_w0, 128)
            pe.sem_inc(ph("n0_evac"), 1)
            with pe.Fori(0, CH) as i:
                pe.wait_ge(ph("n0_dve"), i * NLN + NLN)
                for b in range(CB):
                    last = M.transpose(psf[:, b * P:(b + 1) * P], hs[:, b, :], ident[:, :])
                last.then_inc(ph("n0_transposed"), 1)
                pe.wait_ge(ph("n0_hT"), i + 1)
                pe.wait_ge(ph("n0_evac"), i + 1)
                for b in range(CB):
                    last = M.matmul(psf[:, 1024 + b * P:1024 + (b + 1) * P], hT[:, b * P:(b + 1) * P], w01[:, :],
                                    start=True, stop=True)
                last.then_inc(ph("n0_mm"), 1)
            prefix(1)
            rel_transpose(0)
            pe.wait_ge(s_rele, 1)
            pe.wait_ge(ph("sums_zero"), 1)
            sweep_sums("L0h1", 0, F, True)
            pe.wait_ge(ph("L0h1_kept"), 1)
            sweep_sums("L0h2", 0, 65)


            def transposes():
                for b in range(CB):
                    last = M.transpose(psf[:, b * P:(b + 1) * P], hs[:, b, :], ident[:, :])
                return last

            def by_block(weights):
                for b in range(CB):
                    last = M.matmul(psf[:, 1024 + b * P:1024 + (b + 1) * P], hT[:, b * P:(b + 1) * P], weights,
                                    start=True, stop=True)
                return last

            def by_nodes(at, pairs):
                for c, w in ((0, 512), (512, CN - 512)):
                    for n, (wt, mv) in enumerate(pairs):
                        last = M.matmul(psf[:, at + c:at + c + w], wt, mv(c, w), start=n == 0, stop=n == len(pairs) - 1)
                return last

            pe.wait_ge(s_wt, NWT * 16)
            with pe.Fori(0, CH) as i:
                pe.wait_ge(ph("n1_dve"), i * (NLN + 3) + NLN)
                transposes().then_inc(ph("n1_transposed"), 1)
                pe.wait_ge(ph("n1_hT"), i + 1)
                by_block(wlin[:, :]).then_inc(ph("n1_mm"), 1)
                by_nodes(2048, [(wlin[:, :], lambda c, w: hT[:, c:c + w])]).then_inc(ph("n1_xlT"), 1)
                pe.wait_ge(ph("n1_xlTe"), i + 1)
                for b in range(CB):
                    last = M.matmul(psf[:, 3072 + b * 8:3072 + b * 8 + 8], xlT[:, b * P:(b + 1) * P], watt[:, :], start=True, stop=True)
                last.then_inc(ph("n1_att"), 1)

            def look_up_small(name, i, h, blocks, table, width, one_hots=ohTb, bank=7):
                pe.wait_ge(sig(name, "_ohT"), nth(name, i) * 2 + h + 3)
                pe.wait_ge(sig(name, "_read"), nth(name, i) * 2 + h + 1)
                for k in range(HU):
                    last = M.matmul(ps[:, bank, k * width:(k + 1) * width].unsqueeze(1), one_hots[:, h, k * P:(k + 1) * P],
                                    table[:, ds(blocks[k], 1), :], start=True, stop=True)
                last.then_inc(sig(name, "_looked"), 1)

            def blocks_of(o, i, h):
                return loaded_blocks(mybir.EngineType.PE, o, i, h)

            def look_up(name, o, i, h, table, width, bank=7):
                look_up_small(name, i, h, blocks_of(o, i, h), table, width, bank=bank)

            def sweep_maxima(name, o, table):
                H = heads[name]
                nq = name + "q"
                w = H * P
                R3 = 3 * HU * H
                NS = 6
                credit(pe, name, "_reduced", 2)
                if name != "L1A":
                    credit(pe, nq, "_summed", 4)
                if name == "L2A":
                    credit(pe, nq, "_read", 1)
                    credit(pe, nq, "_looked", 2)
                pe.wait_ge(ph("max_constants"), MAXES.index(name) + 1)

                def turn(i, h):
                    pe.wait_ge(sig(name, "_dve"), (nth(name, i) * 2 + h + 1) * NS)
                    M.matmul(ps[0:R3, 6, 0:P], score3[:, h, 0:R3], ident_b[:, :], start=True, stop=True)\
                        .then_inc(sig(name, "_turned"), 1)

                def tile_max(i, h, k):
                    if k == 0:
                        pe.wait_ge(sig(name, "_masks"), nth(name, i) * 2 + h + 1)
                        pe.wait_ge(sig(name, "_spread"), nth(name, i) * 2 + h + 1)
                    pe.wait_ge(sig(name, "_reduced"), nth(name, i) * U + h * HU + k + 1)
                    M.matmul(ps[:, 4 + k % 2, 0:w].rearrange("p (h e) -> p h e", h=H), ohm[:, h * HU + k, :],
                             low_id.unsqueeze(1).to_broadcast([P, H, P]), start=True, stop=False)
                    M.matmul(ps[:, 4 + k % 2, 0:w], pick[0:R3, k, :], spread[0:R3, h, 0:w], start=False, stop=True)\
                        .then_inc(sig(name, "_maxed"), 1)

                def half(i, h, first, last):
                    if table is None:
                        if not first:
                            turn(*before(i, h))
                            for k in range(HU):
                                tile_max(*before(i, h), k)
                        return
                    blocks = blocks_of(o, i, h)
                    for k in range(HU):
                        t = h * HU + k
                        if k == 0:
                            pe.wait_ge(sig(nq, "_ohT"), nth(nq, i) * 2 + h + 3)
                        pe.wait_ge(sig(nq, "_summed"), nth(nq, i) * U + t + 1)
                        M.matmul(ps[:, k % 4, 0:w].unsqueeze(1), ohT[:, h, k * P:(k + 1) * P], table(blocks[k]),
                                 start=True, stop=True).then_inc(sig(nq, "_q"), 1)
                        if k < 3 and not (isinstance(i, int) and i == 0):
                            tile_max(i - 1, h, k + 5)
                        if k == 1 and not first:
                            turn(*before(i, h))
                        if k == 2 and name == "L2A":
                            look_up_small(nq, i, h, blocks, node12.rearrange("p b c f -> p b (c f)"), 12, ohTq)
                        if k >= 3 and not first:
                            tile_max(*before(i, h), k - 3)

                passes(pe, half)
                if name != "L1A":
                    for k in range(5, HU):
                        tile_max(G - 1, 0, k)
                turn(G - 1, 1)
                for k in range(HU):
                    tile_max(G - 1, 1, k)

            pe.wait_ge(ph("n1_done"), 1)
            sweep_maxima("L1A", 0, None)

            pe.wait_ge(ph("L1B_tables"), 1)
            for what in ("_product", "_looked"):
                credit(pe, "L1B", what, 2)
                credit(pe, "L1C", what, 2)
            credit(pe, "L1B", "_read", 1)
            credit(pe, "L1C", "_read", 1)
            M.matmul(ps[:, 4, 0:13 * NB], zero_b[:, 0:P], zero_b[:, 0:13 * NB], start=True, stop=False)

            def sums_b(i, h):
                blocks = blocks_of(0, i, h)
                pe.wait_ge(sig("L1B", "_onehot"), nth("L1B", i) * 2 + h + 1)
                pe.wait_ge(ph("L1B_dve"), i * 16 + h * 8 + 8)
                for k in range(h * HU, (h + 1) * HU):
                    b = blocks[k % HU]
                    last = M.matmul(ps[:, 4, ds(b * 13, 13)], ohm[:, k, :], p3[:, k, :], start=False, stop=False)
                last.then_inc(sig("L1B", "_product"), 1)

            table = node24.rearrange("p b c f -> p b (c f)")
            ahead(pe, lambda i, h: look_up("L1B", 0, i, h, table, 24), sums_b)
            M.matmul(ps[:, 4, 0:13 * NB], zero_b[:, 0:P], zero_b[:, 0:13 * NB], start=False, stop=True).then_inc(ph("L1B_closed"), 1)

            def sums_c(i, h):
                blocks = blocks_of(1, i, h)
                pe.wait_ge(ph("L1C_wide"), i * 2 + h + 1)
                pe.wait_ge(ph("L1C_dve"), i * 10 + h * 5 + 5)
                for k in range(h * HU, (h + 1) * HU):
                    b = blocks[k % HU]
                    M.matmul(ps[:, 6, ds(b + F, 1)], ohm[:, k, :], p3[:, 0, 12:13], start=False, stop=False)
                    last = M.matmul(psum_blocks[:, ds(b, 1), :], oh[:, k, :], ring[:, k, 0:F].unsqueeze(1), start=False, stop=False)
                last.then_inc(sig("L1C", "_product"), 1)

            table12 = node12.rearrange("p b c f -> p b (c f)")
            pe.wait_ge(ph("n1_sums"), 1)
            rel_transpose(1)
            pe.wait_ge(s_rele, 2)
            open_sums(7, True, F + NB)
            ahead(pe, lambda i, h: look_up("L1C", 1, i, h, table12, 12), sums_c)
            open_sums(7, False, F + NB).then_inc(ph("L1C_closed"), 1)

            pe.wait_ge(ph("L1C_kept"), 1)
            pe.wait_ge(ph("wraw"), 32)
            for h in range(4):
                M.transpose(ps[:, 0, h * P:(h + 1) * P], wk1[:, h * P:(h + 1) * P], ident[:, :])
            for h in range(2):
                last = M.transpose(ps[:, 1, h * P:(h + 1) * P], w3[:, h * P:(h + 1) * P], ident[:, :])
            last.then_inc(s_wT, 1)
            pe.wait_ge(s_wTe, 1)
            with pe.Fori(0, CH) as i:
                pe.wait_ge(ph("n2_dve"), i * (NLN + 16) + NLN)
                transposes().then_inc(ph("n2_transposed"), 1)
                pe.wait_ge(ph("n2_hT"), i * 2 + 2)
                for h in range(4):
                    at = 1024 * (1 + h % 2)
                    by_nodes(at, [(wq1[:, h * P:(h + 1) * P], lambda c, w: hT[:, c:c + w])]).then_inc(ph("n2_q"), 1)
                    pe.wait_ge(ph("n2_qT"), i * 4 + h + 1)
                    if h:
                        pe.wait_ge(ph("n2_dve"), i * (NLN + 16) + NLN + 4 * h)
                    for b in range(CB):
                        c = (b % 3) * 129
                        last = M.matmul(ps[:, 6 + b // 3, c:c + 129], qT[:, h % 2, b * P:(b + 1) * P], wkT[:, h, :], start=True, stop=True)
                    last.then_inc(ph("n2_qk"), 1)

            def sweep_values(name):
                H = heads[name]
                w = 3 * H
                credit(pe, name, "_read", 1)
                credit(pe, name, "_looked", 2)
                credit(pe, name, "_freed", 2)
                pe.wait_ge(ph("values_ready"), nth(name, G) // G)
                M.matmul(ps[:, 7, 0:w * NB], zero_b[:, 0:P], zero_b[:, 0:w * NB], start=True, stop=False)

                def products(i, h, nxt):
                    blocks = blocks_of(1, i, h)
                    pe.wait_ge(sig(name, "_wide"), nth(name, i) * 2 + h + 1)
                    for k in range(h * HU, (h + 1) * HU):
                        if nxt and k % HU == 4:
                            look_up(name, 1, *nxt, mx12[:, :, 0:w], w, 6)
                        pe.wait_ge(sig(name, "_value"), nth(name, i) * U + k + 1)
                        pe.wait_ge(sig(name, "_added"), nth(name, i) * U + k + 1)
                        M.matmul(ps[:, k % 4, 0:H * P], oh[:, k, :], wide[:, k % 2, 0:H * P], start=True, stop=True)\
                            .then_inc(sig(name, "_freed"), 1)
                        if k % HU == 0:
                            pe.wait_ge(sig(name, "_dve"), (nth(name, i) * 2 + h + 1) * 6)
                        M.matmul(ps[:, 7, ds(blocks[k % HU] * w, w)], ohm[:, k, :], p3[:, k, 0:w], start=False, stop=False)\
                            .then_inc(sig(name, "_product"), 1)

                look_up(name, 1, 0, 0, mx12[:, :, 0:w], w, 6)
                with_next(pe, products)
                M.matmul(ps[:, 7, 0:w * NB], zero_b[:, 0:P], zero_b[:, 0:w * NB], start=False, stop=True)\
                    .then_inc(sig(name, "_closed"), 1)

            pe.wait_ge(ph("n2_free"), 1)
            sweep_maxima("L2A", 1, lambda b: big[:, ds(b, 1), :])
            sweep_values("L2C")
            pe.wait_ge(ph("wl2_scaled"), 1)
            pe.sem_inc(ph("n2b_fl"), 1)
            pe.sem_inc(ph("n2b_evac"), 2)
            with pe.Fori(0, CH) as i:
                first = i * (4 + 3 * CB)
                pe.wait_ge(ph("n2b_dve"), first + 4)
                for h in range(4):
                    if h:
                        pe.wait_ge(ph("n2b_aTe"), i * 4 + h)
                    for b in range(CB):
                        last = M.transpose(psf[:, b * P:(b + 1) * P], an[:, b, h, :], ident[:, :])
                    last.then_inc(ph("n2b_aT"), 1)
                for b in range(CB):
                    last = M.transpose(psf[0:4, 1024 + b * P:1024 + (b + 1) * P], stb[:, CB + b, :], ident[:, :])
                last.then_inc(ph("n2b_fl"), 1)
                pe.wait_ge(ph("n2b_aTe"), i * 4 + 4)
                pe.wait_ge(ph("n2b_flT"), i + 1)
                for h in range(4):
                    if h:
                        pe.wait_ge(ph("n2b_h1"), i * 4 + h)
                    by_nodes(2048, [(wv1[:, h * P:(h + 1) * P], lambda c, w: aT[:, h, c:c + w]),
                                    (ws1[:, h * P:(h + 1) * P], lambda c, w: h2T[:, ds(i * CN + c, w)]),
                                    (bv4[:, h, :], lambda c, w: flT[0:4, c:c + w])]).then_inc(ph("n2b_o"), 1)
                pe.wait_ge(ph("n2b_h1"), i * 4 + 4)
                for b in range(CB):
                    pe.wait_ge(ph("n2b_evac"), i * CB + b + 1)
                    first_bank = 6 * (b % 2)
                    for h in range(4):
                        M.matmul(ps[:, first_bank, :], h1T[:, h, b * P:(b + 1) * P], wl2[:, h, 0:512], start=h == 0, stop=h == 3)
                    for h in range(4):
                        last = M.matmul(ps[:, first_bank + 1, 0:384], h1T[:, h, b * P:(b + 1) * P], wl2[:, h, 512:896], start=h == 0, stop=h == 3)
                    last.then_inc(ph("n2b_mm"), 1)
            pe.wait_ge(ph("n2b_free"), 1)
            sweep_maxima("L2D", 1, lambda b: q2[:, ds(b, 1), :])
            sweep_values("L2F")

            with pe.Fori(0, CH) as i:
                pe.wait_ge(ph("n3_dve"), i * (2 * NLN + 4) + 2 * NLN + 1)
                transposes().then_inc(ph("n3_transposed"), 1)
                pe.wait_ge(ph("n3_hT"), i + 1)
                by_block(w3T[:, 0, :]).then_inc(ph("n3_mm"), 1)
            pe.wait_ge(ph("sums_zero"), 2)
            sweep_sums("L3", 1, F)
            with pe.Fori(0, CH) as i:
                pe.wait_ge(ph("n4_dve"), i * 2 + 1)
                transposes().then_inc(ph("n4_transposed"), 1)
                pe.wait_ge(ph("n4_hT"), i + 1)
                by_block(w3T[:, 1, :]).then_inc(ph("n4_mm"), 1)


_INS = ['x', 'src', 'dst', 'edge_weight', 'L0_gnn_W0', 'L0_gnn_b0', 'L0_gnn_W1', 'L0_gnn_b1', 'L0_gnn_fc0', 'L0_gnn_bf0', 'L0_gnn_fc1', 'L0_gnn_bf1', 'L1_gnn_W_lin', 'L1_gnn_b_lin', 'L1_gnn_W_att', 'L1_gnn_b_att', 'L2_gnn_Wq1', 'L2_gnn_bq1', 'L2_gnn_Wk1', 'L2_gnn_bk1', 'L2_gnn_Wv1', 'L2_gnn_bv1', 'L2_gnn_Ws1', 'L2_gnn_bs1', 'L2_gnn_Wq2', 'L2_gnn_bq2', 'L2_gnn_Wk2', 'L2_gnn_bk2', 'L2_gnn_Wv2', 'L2_gnn_bv2', 'L2_gnn_Ws2', 'L2_gnn_bs2', 'L3_gnn_ln_gamma', 'L3_gnn_ln_beta', 'L3_gnn_W', 'L3_gnn_b']


def kernel(**inputs):
    import numpy as _np
    import concourse.bacc as _bacc
    from concourse import mybir as _mybir
    from concourse.bass_utils import run_bass_kernel_spmd as _run

    nc = _bacc.Bacc("TRN2", target_bir_lowering=False, num_devices=1)
    arrays, args = {}, {}
    for name in _INS:
        v = _np.ascontiguousarray(inputs[name])
        arrays[f"in_{name}_dram"] = v
        args[name] = nc.dram_tensor(f"in_{name}_dram", v.shape, _mybir.dt.from_np(v.dtype), kind="ExternalInput").ap()
    out = nc.dram_tensor("out_0_dram", inputs["x"].shape, _mybir.dt.float32, kind="ExternalOutput").ap()
    gnn_stack(nc, args, out)
    r = _run(nc, [arrays], core_ids=[0])
    return r.results[0]["out_0_dram"]
```
